# Optimizing a Trainium2 kernel written in Bass

```python
import numpy as np
import jax
import jax.numpy as jnp

def _softmax(x, axis=-1):
    return jax.nn.softmax(x, axis=axis)

def _gelu(x):
    return jax.nn.gelu(x, approximate=True)

def _silu(x):
    return jax.nn.silu(x)

def _sigmoid(x):
    return jax.nn.sigmoid(x)

def _layernorm(x, axis=-1, eps=1e-05):
    m = jnp.mean(x, axis=axis, keepdims=True)
    v = jnp.var(x, axis=axis, keepdims=True)
    return (x - m) / jnp.sqrt(v + eps)

def _scatter_add(tgt, idx, src, axis=0):
    return tgt.at[idx].add(src)

def _segment_sum(src, seg, n):
    return jax.ops.segment_sum(src, seg, n)
kernel_name = 'mk_gnn_resnorm_d1_gnn_r32_e8a216'

def setup_inputs(seed: int=0):
    np.random.seed(seed)
    _w = jnp.asarray

    def _rec_inputs():
        import jax
        import jax.numpy as jnp
        _gk = jax.random.key(seed)
        x = -0.0005121 + 1.001 * jax.random.normal(jax.random.fold_in(_gk, 1), (3125, 64), jnp.float32)
        _s = jax.random.randint(jax.random.fold_in(_gk, 2), (25000,), 0, 3125, jnp.int32)
        _d = jax.random.randint(jax.random.fold_in(_gk, 3), (25000,), 0, 3125, jnp.int32)
        _loop = jnp.arange(3125, dtype=jnp.int32)
        src = jnp.concatenate([_s, _d, _loop])
        dst = jnp.concatenate([_d, _s, _loop])
        _o = jnp.argsort(dst, stable=True)
        src = src[_o]
        dst = dst[_o]
        edge_weight1 = jax.random.uniform(jax.random.fold_in(_gk, 12), (53125, 1), jnp.float32, 0.0, 0.999999)
        return (x, src, dst, edge_weight1)
    x, src, dst, edge_weight1 = _rec_inputs()

    def _L0_gnn_setup():
        import jax, jax.numpy as jnp
        import numpy as np
        N_NODES = 50000
        N_EDGES = 25000
        NODE_NF = 64
        HIDDEN_NF = 128

        def _linear_params(key, fan_in, fan_out):
            kw, kb = jax.random.split(key)
            bound = 1.0 / np.sqrt(fan_in)
            W = jax.random.uniform(kw, (fan_in, fan_out), minval=-bound, maxval=bound, dtype=jnp.float32)
            b = jax.random.uniform(kb, (fan_out,), minval=-bound, maxval=bound, dtype=jnp.float32)
            return (W, b)
        key = jax.random.key(seed)
        ks = jax.random.split(key, 8)
        h = jax.random.normal(ks[0], (N_NODES, NODE_NF), dtype=jnp.float32)
        row = jax.random.randint(ks[1], (N_EDGES,), 0, N_NODES)
        col = jax.random.randint(ks[2], (N_EDGES,), 0, N_NODES)
        dist = jax.random.uniform(ks[3], (N_EDGES, 1), dtype=jnp.float32)
        eW1, eb1 = _linear_params(ks[4], 2 * NODE_NF + 1, HIDDEN_NF)
        eW2, eb2 = _linear_params(ks[5], HIDDEN_NF, HIDDEN_NF)
        nW1, nb1 = _linear_params(ks[6], HIDDEN_NF + NODE_NF, HIDDEN_NF)
        nW2, nb2 = _linear_params(ks[7], HIDDEN_NF, NODE_NF)
        return {'h': h, 'row': row, 'col': col, 'dist': dist, 'eW1': eW1, 'eb1': eb1, 'eW2': eW2, 'eb2': eb2, 'nW1': nW1, 'nb1': nb1, 'nW2': nW2, 'nb2': nb2}
    _L0_gnn_all = _L0_gnn_setup()
    _L0_gnn_in = {k: v for k, v in _L0_gnn_all.items() if k in ('eW1', 'eb1', 'eW2', 'eb2', 'nW1', 'nb1', 'nW2', 'nb2')}
    del _L0_gnn_all
    return {'x': x, 'src': src, 'dst': dst, 'edge_weight1': edge_weight1, 'L0_gnn_eW1': _L0_gnn_in['eW1'], 'L0_gnn_eb1': _L0_gnn_in['eb1'], 'L0_gnn_eW2': _L0_gnn_in['eW2'], 'L0_gnn_eb2': _L0_gnn_in['eb2'], 'L0_gnn_nW1': _L0_gnn_in['nW1'], 'L0_gnn_nb1': _L0_gnn_in['nb1'], 'L0_gnn_nW2': _L0_gnn_in['nW2'], 'L0_gnn_nb2': _L0_gnn_in['nb2']}

def reference(x, src, dst, edge_weight1, L0_gnn_eW1, L0_gnn_eb1, L0_gnn_eW2, L0_gnn_eb2, L0_gnn_nW1, L0_gnn_nb1, L0_gnn_nW2, L0_gnn_nb2):
    import jax
    import jax.numpy as jnp

    def _L0_gnn_ref(h, row, col, dist, eW1, eb1, eW2, eb2, nW1, nb1, nW2, nb2):
        import jax, jax.numpy as jnp
        import numpy as np
        N_NODES = 50000
        N_EDGES = 25000
        NODE_NF = 64
        HIDDEN_NF = 128

        def _linear_params(key, fan_in, fan_out):
            kw, kb = jax.random.split(key)
            bound = 1.0 / np.sqrt(fan_in)
            W = jax.random.uniform(kw, (fan_in, fan_out), minval=-bound, maxval=bound, dtype=jnp.float32)
            b = jax.random.uniform(kb, (fan_out,), minval=-bound, maxval=bound, dtype=jnp.float32)
            return (W, b)
        edge_in = jnp.concatenate([h[row], h[col], dist], axis=1)
        e = jax.nn.silu(edge_in @ eW1 + eb1)
        e = jax.nn.silu(e @ eW2 + eb2)
        agg = jax.ops.segment_sum(e, row, num_segments=h.shape[0])
        node_in = jnp.concatenate([h, agg], axis=1)
        out = jax.nn.silu(node_in @ nW1 + nb1) @ nW2 + nb2
        return out
    x = _layernorm(x + _L0_gnn_ref(x, src, dst, edge_weight1, L0_gnn_eW1, L0_gnn_eb1, L0_gnn_eW2, L0_gnn_eb2, L0_gnn_nW1, L0_gnn_nb1, L0_gnn_nW2, L0_gnn_nb2), axis=-1)
    return x

_drawn_inputs = setup_inputs


def setup_inputs(seed=0):
    import zlib

    import numpy as np

    out = dict(_drawn_inputs(seed))
    spreads = {}
    factors = {'edge_weight1': 39.441, 'L0_gnn_nb1': 4.257}
    for name, (base, spread) in spreads.items():
        noise = np.random.default_rng([zlib.crc32(name.encode()), seed]).standard_normal(out[name].shape)
        drawn = base * np.exp(spread * noise) if base else spread * noise
        out[name] = jnp.asarray(drawn.astype(out[name].dtype))
    for name, factor in factors.items():
        out[name] = (out[name] * factor).astype(out[name].dtype)
    return out
```

```python
from contextlib import ExitStack

import concourse.bass as bass
from concourse import mybir

F32 = mybir.dt.float32
BF16 = mybir.dt.bfloat16
I32 = mybir.dt.int32
ALU = mybir.AluOpType
ACT = mybir.ActivationFunctionType
AX = mybir.AxisListType
ENG = mybir.EngineType

NODES, NF, HID = 3125, 64, 128
EDGES = 53125
LO = 125
WIN = NODES // LO
EP = 125
ECOL = EDGES // EP
SLOT = 128
GT = 4
UNROLL = 4
SORTS = 5
LOAD = [65, 120, 120, 120]
EPS = 1e-5
ROUND = 1.5 * 2.0 ** 23
KEY = 128
SPLITS = 3


def sorted_tiles(cols):
    worst = (EP * cols + WIN * (SLOT - 1)) // SLOT
    step = GT * UNROLL
    return -(-worst // step) * step


TILES = [sorted_tiles(s) for s in LOAD]
CHUNKS = len(LOAD)
COL0 = [sum(LOAD[:k]) for k in range(CHUNKS)]
GRP0 = [sum(TILES[:k]) // GT for k in range(CHUNKS)]
ALL_TILES = sum(TILES)
GROUPS = ALL_TILES // GT
CMAX, SMAX = max(TILES), max(LOAD)
assert SMAX <= 2 * NF and sum(LOAD) == ECOL and EP * ECOL == EDGES and LO * WIN == NODES
assert all(s % SORTS == 0 and s // SORTS % UNROLL == 0 and s // SORTS <= c // GT
           for s, c in zip(LOAD[1:], TILES)) and 2 * CMAX <= 512

XT_W = 4
LN_W = 5


LATE = 99


def spans(n, step):
    return [(a, min(a + step, n)) for a in range(0, n, step)]


def build(nc, x, src, dst, edge_weight, eW1, eb1, eW2, eb2, nW1, nb1, nW2, nb2, out):
    with ExitStack() as ctx:
        def sb(name, shape, dt=F32):
            return ctx.enter_context(nc.sbuf_tensor(name, shape, dt))

        def ps(name, shape, dt=F32):
            return ctx.enter_context(nc.psum_tensor(name, shape, dt))

        def sem(name):
            return ctx.enter_context(nc.semaphore(name))

        q_table = nc.dram_tensor("q_table", [NODES, HID], F32).ap()

        iota_i = sb("iota_i", [128, CMAX], I32)
        part_i = sb("part_i", [128, 1], I32)
        iota_f = sb("iota_f", [128, CMAX])
        iota1_f = sb("iota1_f", [128, 128])
        part_f = sb("part_f", [128, 1])
        lo_plus1 = sb("lo_plus1", [128, LO], BF16)
        ident_f = sb("ident_f", [128, 128])
        ident_b = sb("ident_b", [128, 128], BF16)
        before = sb("before", [128, 128])
        upto = sb("upto", [WIN, WIN])
        ones = sb("ones", [128, 128])
        zeros = sb("zeros", [128, 512])
        ones3 = sb("ones3", [128, 128], BF16)
        keep = {n: sb(f"keep{n}", [EP, WIN, n], BF16) for n in sorted(set(LOAD))}
        w1_sb = sb("w1_sb", [NF + 1, 2 * HID])
        w2_sb = sb("w2_sb", [HID, HID])
        b2_in = sb("b2_in", [SPLITS, HID])
        b2_part = sb("b2_part", [SPLITS, HID], BF16)
        b2_work = sb("b2_work", [SPLITS, 2, HID])
        b2_rows = sb("b2_rows", [128, GT, HID], BF16)
        n1x_sb = sb("n1x_sb", [NF, HID])
        n1a_sb = sb("n1a_sb", [HID, HID])
        nb1_sb = sb("nb1_sb", [HID, 1])
        n2_sb = sb("n2_sb", [HID, NF])
        res_sb = sb("res_sb", [NF + 1, NF])
        wc_in = sb("wc_in", [128, HID])
        wc_part = sb("wc_part", [128, SPLITS, HID], BF16)
        wc_rest = sb("wc_rest", [128, SPLITS, HID])
        x_sb = sb("x_sb", [LO, WIN * NF])
        xT = sb("xT", [NF + 1, NODES])
        pq = sb("pq", [128, WIN * 2 * HID])
        p_table = sb("p_table", [128, WIN, SPLITS, HID], BF16)
        sums = [sb(f"sums{i}", [HID, WIN * HID]) for i in range(2)]
        agg = [t[:, 0:NODES] for t in sums]
        rest = sums[1][0:LO, :]
        src_i = sb("src_i", [EP, ECOL], I32)
        dst_i = sb("dst_i", [EP, ECOL], I32)
        w_in = sb("w_in", [EP, ECOL])
        src_f = sb("src_f", [EP, ECOL])
        lo_f = sb("lo_f", [EP, ECOL])
        win_f = sb("win_f", [EP, ECOL])
        payload = sb("payload", [EP, ECOL, 2])
        in_win = sb("in_win", [EP, WIN * SMAX], BF16)
        count = sb("count", [EP, WIN * SMAX], BF16)
        scratch = sb("scratch", [EP, 2 * WIN * NF])
        place = scratch
        slot = sb("slot", [EP, SMAX])
        slot_t = sb("slot_t", [EP, SMAX])
        col_s = sb("col_s", [EP, SMAX])
        row_s = sb("row_s", [EP, SMAX])
        small = sb("small", [128, 12, WIN])
        ge = sb("ge", [WIN, CMAX])
        row_hot = sb("row_hot", [EP, 4, SLOT])
        col_hot = sb("col_hot", [EP, 4, 2, CMAX])
        key_s = sb("key_s", [128, CMAX])
        slot_k = sb("slot_k", [128, CMAX])
        w_s = sb("w_s", [128, 3, CMAX])
        dst_f = sb("dst_f", [128, CMAX])
        lo1 = sb("lo1", [128, ALL_TILES])
        w_parts = sb("w_parts", [128, ALL_TILES, SPLITS], BF16)
        q_index = sb("q_index", [128, ALL_TILES], I32)
        rows_at = sb("rows_at", [128, 4, GT], I32)
        p_at = sb("p_at", [1, ALL_TILES], I32)
        agg_at = sb("agg_at", [1, ALL_TILES], I32)
        q_rows = sb("q_rows", [128, 4, GT, HID])
        hot = sb("hot", [128, 2, GT, 128], BF16)
        hot32 = sb("hot32", [128, 4, GT, LO])
        hotT = sb("hotT", [128, 2, GT * 128], BF16)
        h1 = sb("h1", [HID, 2, GT * 128])
        e2 = sb("e2", [128, 2, GT * HID])
        hT = pq
        yc = scratch[:, 0:WIN * NF].rearrange("p (b f) -> p b f", b=WIN)
        sq = scratch[:, WIN * NF:2 * WIN * NF].rearrange("p (b f) -> p b f", b=WIN)
        stat = sb("stat", [LO, 4, WIN])

        sort_ps = ps("sort_ps", [128, 512])
        hotT_ps = [ps(f"hotT_ps{i}", [128, GT * 128], BF16) for i in range(2)]
        pre_ps = [ps(f"pre_ps{i}", [128, 512]) for i in range(2)]
        e_ps = [ps(f"e_ps{i}", [128, 512]) for i in range(2)]
        seg_ps = ps("seg_ps", [128, 512])
        y_banks = [sort_ps, seg_ps]
        work_ps = [pre_ps[0], pre_ps[1], e_ps[0], e_ps[1]]

        src_in, dst_in, w_in_sem, x_in, w_loaded, wc_loaded = (
            sem(n) for n in ("src_in", "dst_in", "w_in_sem", "x_in", "w_loaded", "wc_loaded"))
        iotas_ready = sem("iotas_ready")
        fills_ready = sem("fills_ready")
        v_done = sem("v_done")
        s_done = sem("s_done")
        ident_ready = sem("ident_ready")
        xT_ps_ready = sem("xT_ps_ready")
        xT_copied = sem("xT_copied")
        pq_ps_ready = sem("pq_ps_ready")
        pq_copied = sem("pq_copied")
        wc_step = sem("wc_step")
        wc_placed = sem("wc_placed")
        p_part = sem("p_part")
        p_rest = sem("p_rest")
        q_stored = sem("q_stored")
        b2_ready = sem("b2_ready")
        totals_ready = sem("totals_ready")
        offsets_ready = sem("offsets_ready")
        pads_ready = sem("pads_ready")
        ends_ready = sem("ends_ready")
        ge_ready = sem("ge_ready")
        window_ready = sem("window_ready")
        slots_ready = sem("slots_ready")
        hots_ready = sem("hots_ready")
        sort_mm = sem("sort_mm")
        sorted_ready = sem("sorted_ready")
        tables_ready = sem("tables_ready")
        rows_in = [sem(f"rows_in{i}") for i in range(4)]
        staged = sem("staged")
        hot_ready = sem("hot_ready")
        hotT_ps_ready = sem("hotT_ps_ready")
        hot32_ready = sem("hot32_ready")
        hotT_ready = sem("hotT_ready")
        pre_ready = sem("pre_ready")
        h1_ready = sem("h1_ready")
        e_ready = sem("e_ready")
        e2_ready = sem("e2_ready")
        seg_ready = sem("seg_ready")
        agg_added = sem("agg_added")
        agg_whole = sem("agg_whole")
        hid_ps_ready = sem("hid_ps_ready")
        hid_ready = sem("hid_ready")
        y_ready = sem("y_ready")
        y_read = sem("y_read")
        ln_var = sem("ln_var")
        ln_sd = sem("ln_sd")
        ln_done = sem("ln_done")
        out_stored = sem("out_stored")

        xt_spans, ln_spans = spans(WIN, XT_W), spans(WIN, LN_W)
        pq_spans = spans(WIN, 2)

        def seg(ap3, b0, b1):
            return ap3[:, b0:b1, :]

        FILLS = 7 + 2 * len(keep)

        block = ctx.enter_context(nc.Block())

        @block.sync
        def _(sp):
            sp.dma_start(src_i[:], src.rearrange("(p t) -> p t", p=EP)).then_inc(src_in, 16)
            sp.dma_start(dst_i[:], dst.rearrange("(p t) -> p t", p=EP)).then_inc(dst_in, 16)
            sp.dma_start(w_in[:], edge_weight.rearrange("(p t) o -> p (t o)", p=EP)).then_inc(w_in_sem, 16)
            sp.wait_ge(pq_copied, len(pq_spans))
            sp.dma_start(q_table.rearrange("(p b) f -> p b f", b=WIN),
                         pq[0:LO, :].rearrange("p (b h) -> p b h", b=WIN)[:, :, HID:2 * HID]).then_inc(q_stored, 16)
            for n, (b0, b1) in enumerate(ln_spans):
                sp.wait_ge(ln_done, n + 1)
                sp.dma_start(out.rearrange("(p b) f -> p b f", b=WIN)[:, b0:b1, :],
                             seg(yc, b0, b1)).then_inc(out_stored, 16)
            sp.wait_ge(out_stored, 16 * len(ln_spans))

        W_LOADS = 10

        @block.scalar
        def _(act):
            act.dma_start(x_sb[:], x.rearrange("(p b) f -> p (b f)", b=WIN)).then_inc(x_in, 16)
            act.dma_start(w1_sb[0:NF, 0:HID], eW1[0:NF, :]).then_inc(w_loaded, 16)
            act.dma_start(w1_sb[0:NF, HID:2 * HID], eW1[NF:2 * NF, :]).then_inc(w_loaded, 16)
            act.dma_start(w1_sb[NF:NF + 1, 0:HID], eb1.rearrange("(a f) -> a f", a=1)).then_inc(w_loaded, 16)
            act.dma_start(wc_in[96:128, :], eW1[2 * NF:2 * NF + 1, :].to_broadcast([32, HID])).then_inc(wc_loaded, 16)
            act.dma_start(b2_in[:], eb2.rearrange("(a f) -> a f", a=1).to_broadcast([SPLITS, HID])).then_inc(w_loaded, 16)
            act.dma_start(w2_sb[:], eW2).then_inc(w_loaded, 16)
            act.dma_start(n1x_sb[:], nW1[0:NF, :]).then_inc(w_loaded, 16)
            act.dma_start(n1a_sb[:], nW1[NF:NF + HID, :]).then_inc(w_loaded, 16)
            act.dma_start(nb1_sb[:], nb1.rearrange("(f a) -> f a", a=1)).then_inc(w_loaded, 16)
            act.dma_start(n2_sb[:], nW2).then_inc(w_loaded, 16)
            act.dma_start(res_sb[NF:NF + 1, :], nb2.rearrange("(a f) -> a f", a=1)).then_inc(w_loaded, 16)

            for n, (b0, b1) in enumerate(xt_spans):
                act.wait_ge(xT_ps_ready, n + 1)
                nc.scalar.activation(xT[0:NF, b0 * LO:b1 * LO], work_ps[n % 4][0:NF, 0:(b1 - b0) * LO],
                                     ACT.Copy).then_inc(xT_copied, 1)
            for n, (b0, b1) in enumerate(pq_spans):
                act.wait_ge(pq_ps_ready, n + 1)
                nc.scalar.activation(pq[0:LO, b0 * 2 * HID:b1 * 2 * HID],
                                     work_ps[n % 4][0:LO, 0:(b1 - b0) * 2 * HID], ACT.Copy).then_inc(pq_copied, 1)

            act.wait_ge(wc_placed, SPLITS)
            act.wait_ge(pq_copied, len(pq_spans))
            for s in range(SPLITS):
                if s == 0:
                    left = pq[0:LO, :].rearrange("p (b h) -> p b h", b=WIN)[:, :, 0:HID]
                else:
                    act.wait_ge(p_rest, s)
                    left = rest.rearrange("p (b h) -> p b h", b=WIN)
                nc.scalar.activation(p_table[0:LO, :, s, :], left, ACT.Copy).then_inc(p_part, 1)

            def convert(g, u, n):
                act.wait_ge(hot_ready, 2 * g + 2)
                if n >= 4:
                    act.wait_ge(seg_ready, g - 3)
                nc.scalar.activation(hot32[:, u % 4], hot[:, u % 2, :, 0:LO], ACT.Copy).then_inc(hot32_ready, 1)

            def turned(g, u, n):
                act.wait_ge(hotT_ps_ready, g + 1)
                if n >= 2:
                    act.wait_ge(pre_ready, g - 1)
                nc.scalar.activation(hotT[:, u % 2, :], hotT_ps[u % 2][:], ACT.Copy).then_inc(hotT_ready, 1)

            def silu1(m, u, n):
                act.wait_ge(pre_ready, m + 1)
                if n >= 3:
                    act.wait_ge(e_ready, m - 1)
                nc.scalar.activation(h1[:, u % 2, :], pre_ps[u % 2][:], ACT.Silu).then_inc(h1_ready, 1)

            def silu2(m, u, n):
                act.wait_ge(e_ready, m + 1)
                if n >= 4:
                    act.wait_ge(seg_ready, m - 1)
                nc.scalar.activation(e2[:, u % 2, :], e_ps[u % 2][:], ACT.Silu).then_inc(e2_ready, 1)

            def step(g, u, n):
                convert(g, u, n)
                turned(g, u, n)
                if n >= 1:
                    silu1(g - 1, u + 3, n)
                if n >= 2:
                    silu2(g - 2, u + 2, n)

            for g in range(UNROLL):
                step(g, g, g)
            with act.Fori(UNROLL, GROUPS - (UNROLL - 1), UNROLL) as g:
                for u in range(UNROLL):
                    step(g + u, u, LATE)
            silu1(GROUPS - 1, UNROLL + 3, LATE)
            silu2(GROUPS - 2, UNROLL + 2, LATE)
            silu2(GROUPS - 1, UNROLL + 3, LATE)

            for n, (b0, b1) in enumerate(xt_spans):
                act.wait_ge(hid_ps_ready, n + 1)
                nc.scalar.activation(hT[:, b0 * LO:b1 * LO], work_ps[n % 4][:, 0:(b1 - b0) * LO], ACT.Silu,
                                     bias=nb1_sb[:, 0:1]).then_inc(hid_ready, 1)
            act.wait_ge(ln_var, 1)
            nc.scalar.activation(stat[:, 2, :], stat[:, 1, :], ACT.Sqrt).then_inc(ln_sd, 1)

        @block.gpsimd
        def _(pool):
            nc.gpsimd.iota(iota_i[:], pattern=[[1, CMAX]], base=0, channel_multiplier=0).then_inc(iotas_ready, 1)
            nc.gpsimd.iota(part_i[:], pattern=[[0, 1]], base=0, channel_multiplier=1).then_inc(iotas_ready, 1)
            fills = ([(ones[:], 1.0)] + [(t[:], 1.0) for t in keep.values()] + [(ones3[:], 0.0), (zeros[:], 0.0),
                     (b2_rows[:], 0.0), (w1_sb[NF:NF + 1, HID:2 * HID], 0.0), (xT[NF:NF + 1, :], 1.0),
                     (ones3[0:SPLITS, :], 1.0)] + [(t[:, :, 0:1], 0.0) for t in keep.values()])
            for n, (t, value) in enumerate(fills):
                pool.wait_ge(fills_ready, n)
                nc.gpsimd.memset(t, value).then_inc(fills_ready, 1)
            pool.wait_ge(fills_ready, FILLS)
            nc.gpsimd.memset(agg[0], 0.0).then_inc(agg_added, 1)

            pool.wait_ge(wc_loaded, 16)
            pool.wait_ge(agg_added, 1)
            for s in range(SPLITS):
                left = wc_in[96:128, :] if s == 0 else wc_rest[96:128, s - 1, :]
                nc.gpsimd.tensor_copy(wc_part[96:128, s, :], left).then_inc(wc_step, 1)
                pool.wait_ge(wc_step, 2 * s + 1)
                nc.gpsimd.tensor_tensor(wc_rest[96:128, s, :], left, wc_part[96:128, s, :], ALU.subtract).then_inc(wc_step, 1)
                pool.wait_ge(wc_step, 2 * s + 2)
                nc.gpsimd.tensor_copy(p_table[96:128, :, s, :],
                                      wc_part[96:128, s, :].unsqueeze(1).to_broadcast([32, WIN, HID])).then_inc(wc_placed, 1)
                pool.wait_ge(wc_placed, s + 1)

            for s in range(SPLITS - 1):
                pool.wait_ge(p_part, s + 1)
                left = (pq[0:LO, :].rearrange("p (b h) -> p b h", b=WIN)[:, :, 0:HID] if s == 0
                        else rest.rearrange("p (b h) -> p b h", b=WIN))
                nc.gpsimd.tensor_tensor(rest.rearrange("p (b h) -> p b h", b=WIN), left,
                                        p_table[0:LO, :, s, :], ALU.subtract).then_inc(p_rest, 1)

            pool.wait_ge(p_part, SPLITS)
            nc.gpsimd.memset(agg[1], 0.0).then_inc(agg_added, 1)

            def stage(g, u, n):
                if n >= 4:
                    pool.wait_ge(pre_ready, g - 3)
                at = q_index[:, GT * g:GT * g + GT] if isinstance(g, int) else q_index[:, bass.ds(g * GT, GT)]
                nc.gpsimd.tensor_copy(rows_at[:, u % 4, :], at).then_inc(staged, 1)

            def gather(g, u, n, more):
                pool.wait_ge(staged, g + 1)
                if more:
                    stage(g + 1, u + 1, n + 1)
                for j in range(GT):
                    nc.gpsimd.indirect_dma_start(
                        q_rows[:, u, j, :], None, q_table,
                        bass.IndirectOffsetOnAxis(ap=rows_at[:, u, j:j + 1], axis=0)).then_inc(rows_in[u], 16)

            pool.wait_ge(q_stored, 16)
            for k in range(CHUNKS):
                pool.wait_ge(tables_ready, k + 1)
                g0, g1 = GRP0[k], GRP0[k] + TILES[k] // GT
                stage(g0, 0, g0)
                if k == 0:
                    for u in range(UNROLL):
                        gather(u, u, u, True)
                    g0 += UNROLL
                with pool.Fori(g0, g1 - UNROLL - (UNROLL - 1), UNROLL) as g:
                    for u in range(UNROLL):
                        gather(g + u, u, LATE, True)
                for u in range(UNROLL):
                    gather(g1 - UNROLL + u, u, LATE, u < UNROLL - 1)

        @block.tensor
        def _(pe):
            def mm(o, lhsT, rhs, start, stop, **kw):
                return nc.tensor.matmul(o, lhsT, rhs, start=start, stop=stop, **kw)

            def place_edges(k):
                pe.wait_ge(totals_ready, k + 1)
                tot = small[0:EP, 0, :]
                mm(sort_ps[0:EP, 0:WIN], before[0:EP, 0:EP], tot, True, True)
                mm(sort_ps[0:EP, 32:32 + WIN], ones[0:EP, 0:EP], tot, True, True)
                mm(sort_ps[0:WIN, 64:65], tot, ones[0:EP, 0:1], True, True).then_inc(offsets_ready, 1)
                pe.wait_ge(pads_ready, k + 1)
                mm(sort_ps[0:WIN, 96:97], upto[:], small[0:WIN, 8, 0:1], True, True).then_inc(ends_ready, 1)
                pe.wait_ge(ge_ready, k + 1)
                mm(sort_ps[0:1, 128:128 + TILES[k]], ones[0:WIN - 1, 0:1], ge[0:WIN - 1, 0:TILES[k]],
                   True, True).then_inc(window_ready, 1)

            def sort_open(k):
                pe.wait_ge(slots_ready, k + 1)
                mm(sort_ps[:, 0:2 * TILES[k]], zeros[0:EP, 0:128], zeros[0:EP, 0:2 * TILES[k]], True, False)

            def sort_tile(k, n, b):
                pe.wait_ge(hots_ready, 2 * n + 2)
                mm(sort_ps[:, 0:2 * TILES[k]], row_hot[:, b, :], col_hot[:, b, :, 0:TILES[k]],
                   False, False).then_inc(sort_mm, 1)

            def sort_close(k):
                mm(sort_ps[:, 0:2 * TILES[k]], zeros[0:EP, 0:128], zeros[0:EP, 0:2 * TILES[k]],
                   False, True).then_inc(sorted_ready, 1)

            pe.wait_ge(x_in, 16)
            pe.wait_ge(ident_ready, 1)
            for n, (b0, b1) in enumerate(xt_spans):
                if n >= 4:
                    pe.wait_ge(xT_copied, n - 3)
                for b in range(b0, b1):
                    last = nc.tensor.transpose(work_ps[n % 4][0:NF, (b - b0) * LO:(b - b0 + 1) * LO],
                                               x_sb[:, b * NF:(b + 1) * NF], ident_f[0:LO, 0:LO])
                last.then_inc(xT_ps_ready, 1)
            pe.wait_ge(xT_copied, len(xt_spans))
            pe.wait_ge(w_loaded, 16 * W_LOADS)
            pe.wait_ge(fills_ready, FILLS)
            for n, (b0, b1) in enumerate(pq_spans):
                if n >= 4:
                    pe.wait_ge(pq_copied, n - 3)
                for b in range(b0, b1):
                    last = mm(work_ps[n % 4][0:LO, (b - b0) * 2 * HID:(b - b0 + 1) * 2 * HID],
                              xT[:, b * LO:(b + 1) * LO], w1_sb[:], True, True)
                last.then_inc(pq_ps_ready, 1)

            place_edges(0)
            sort_open(0)
            with pe.Fori(0, LOAD[0] - 1 - (4 - 1), 4) as t:
                for b in range(4):
                    sort_tile(0, t + b, b)
            for t in range((LOAD[0] - 1) // 4 * 4, LOAD[0]):
                sort_tile(0, t, t % 4)
            sort_close(0)
            place_edges(1)

            def turn(g, u, n):
                pe.wait_ge(hot_ready, 2 * g + 2)
                if n >= 2:
                    pe.wait_ge(hotT_ready, g - 1)
                for j in range(GT):
                    last = nc.tensor.transpose(hotT_ps[u % 2][:, j * 128:(j + 1) * 128], hot[:, u % 2, j, :], ident_b[:])
                last.then_inc(hotT_ps_ready, 1)

            def tile_windows(m):
                at = p_at[0:1, GT * m:GT * m + GT] if isinstance(m, int) else p_at[0:1, bass.ds(m * GT, GT)]
                return nc.values_load_multi_w_load_instructions(
                    at, engines=(ENG.PE,), min_val=0, max_val=(WIN - 1) * SPLITS * HID,
                    skip_runtime_bounds_check_because="a window's number is a count of 24 comparisons")[1]

            p_flat = p_table[:].rearrange("p b s f -> p (b s f)")

            def first_layer(m, u, n):
                windows = tile_windows(m)
                pe.wait_ge(rows_in[u % 4], rows_count(m, u))
                pe.wait_ge(hotT_ready, m + 1)
                if n >= 3:
                    pe.wait_ge(h1_ready, m - 1)
                for j in range(GT):
                    o = pre_ps[u % 2][:, j * 128:(j + 1) * 128]
                    mm(o, q_rows[:, u % 4, j, :], ident_f[:], True, False, is_transpose=True)
                    for s in range(SPLITS):
                        last = mm(o, p_flat[:, bass.ds(windows[j] + s * HID, HID)],
                                  hotT[:, u % 2, j * 128:(j + 1) * 128], False, s == SPLITS - 1)
                last.then_inc(pre_ready, 1)

            def rows_count(m, u):
                if isinstance(m, int):
                    return 16 * GT * (m // 4 + 1)
                return (m - u % 4) * (16 * GT // 4) + 16 * GT

            def second_layer(m, u, n):
                pe.wait_ge(h1_ready, m + 1)
                if n >= 4:
                    pe.wait_ge(e2_ready, m - 1)
                mm(e_ps[u % 2][:], ones3[:], b2_rows[:].rearrange("p j f -> p (j f)"), True, False)
                for j in range(GT):
                    last = mm(e_ps[u % 2][:, j * HID:(j + 1) * HID], h1[:, u % 2, j * 128:(j + 1) * 128], w2_sb[:],
                              False, j == GT - 1)
                last.then_inc(e_ready, 1)

            def segment(m, u, n):
                pe.wait_ge(e2_ready, m + 1)
                pe.wait_ge(hot32_ready, m + 1)
                if n >= 4:
                    pe.wait_ge(agg_added, m * GT + 2)
                for j in range(GT):
                    last = mm(seg_ps[:, j * LO:(j + 1) * LO], e2[:, u % 2, j * HID:(j + 1) * HID],
                              hot32[:, u % 4, j, :], True, True)
                last.then_inc(seg_ready, 1)

            def step(g, u, n, k=None, t0=None):
                turn(g, u, n)
                if n >= 1:
                    first_layer(g - 1, u + 3, n)
                if k is not None:
                    for i in range(SORTS):
                        sort_tile(k, t0 + i, (SORTS * u + i) % 4)
                if n >= 2:
                    second_layer(g - 2, u + 2, n)
                if n >= 3:
                    segment(g - 3, u + 1, n)

            pe.wait_ge(p_part, SPLITS)
            pe.wait_ge(b2_ready, 1)
            for k in range(CHUNKS):
                g0, g1 = GRP0[k], GRP0[k] + TILES[k] // GT
                pe.wait_ge(tables_ready, k + 1)
                if k + 1 < CHUNKS:
                    sort_open(k + 1)
                    mixed = g0 + LOAD[k + 1] // SORTS
                else:
                    mixed = g0
                base = COL0[k + 1] if k + 1 < CHUNKS else None
                if k == 0:
                    for u in range(UNROLL):
                        step(u, u, u, 1, base + SORTS * u)
                if mixed > g0:
                    a = g0 + (UNROLL if k == 0 else 0)
                    with pe.Fori(a, mixed - (UNROLL - 1), UNROLL) as g:
                        for u in range(UNROLL):
                            step(g + u, u, LATE, k + 1, g * SORTS + (base + SORTS * (u - g0)))
                    sort_close(k + 1)
                if k + 2 < CHUNKS:
                    place_edges(k + 2)
                if g1 > mixed:
                    with pe.Fori(mixed, g1 - (UNROLL - 1), UNROLL) as g:
                        for u in range(UNROLL):
                            step(g + u, u, LATE)
            u = UNROLL
            first_layer(GROUPS - 1, u + 3, LATE)
            second_layer(GROUPS - 2, u + 2, LATE)
            segment(GROUPS - 3, u + 1, LATE)
            second_layer(GROUPS - 1, u + 3, LATE)
            segment(GROUPS - 2, u + 2, LATE)
            segment(GROUPS - 1, u + 3, LATE)

            for n, (b0, b1) in enumerate(xt_spans):
                o = work_ps[n % 4][:, 0:(b1 - b0) * LO]
                if n >= 4:
                    pe.wait_ge(hid_ready, n - 3)
                else:
                    pe.wait_ge(e2_ready, GROUPS)
                mm(o, n1x_sb[:], xT[0:NF, b0 * LO:b1 * LO], True, False)
                pe.wait_ge(agg_whole, n + 1)
                mm(o, n1a_sb[:], agg[0][:, b0 * LO:b1 * LO], False, True).then_inc(hid_ps_ready, 1)
            for n, (b0, b1) in enumerate(ln_spans):
                pe.wait_ge(hid_ready, -(-b1 // XT_W))
                if n >= len(y_banks):
                    pe.wait_ge(y_read, n - len(y_banks) + 1)
                for b in range(b0, b1):
                    o = y_banks[n % len(y_banks)][0:LO, (b - b0) * NF:(b - b0 + 1) * NF]
                    mm(o, hT[:, b * LO:(b + 1) * LO], n2_sb[:], True, False)
                    last = mm(o, xT[:, b * LO:(b + 1) * LO], res_sb[:], False, True)
                last.then_inc(y_ready, 1)

        @block.vector
        def _(dve):
            V = nc.vector
            steps = [0]

            def then(ins):
                steps[0] += 1
                ins.then_inc(v_done, 1)
                dve.wait_ge(v_done, steps[0])

            def scaled_round(dst, tmp, src, scale, shift):
                then(V.tensor_scalar(tmp, src, scale, shift, ALU.mult, ALU.add))
                then(V.tensor_scalar(dst, tmp, ROUND, -ROUND, ALU.add, ALU.add))

            dve.wait_ge(iotas_ready, 2)
            then(V.tensor_copy(iota_f[:], iota_i[:]))
            then(V.tensor_copy(part_f[:], part_i[:]))
            V.tensor_scalar(ident_f[:], iota_f[:, 0:128], part_f[:, 0:1], None, ALU.is_equal).then_inc(ident_ready, 1)
            dve.wait_ge(ident_ready, 1)
            then(V.tensor_copy(ident_b[:], ident_f[:]))
            then(V.tensor_scalar(before[:], iota_f[:, 0:128], part_f[:, 0:1], None, ALU.is_gt))
            then(V.tensor_scalar(upto[:], iota_f[0:WIN, 0:WIN], part_f[0:WIN, 0:1], None, ALU.is_ge))
            then(V.tensor_scalar(iota1_f[:], iota_f[:, 0:128], 1.0, None, ALU.add))
            then(V.tensor_copy(lo_plus1[:], iota1_f[:, 0:LO]))

            dve.wait_ge(src_in, 16)
            then(V.tensor_copy(src_f[:], src_i[:]))
            scaled_round(lo_f[:], win_f[:], src_f[:], 1.0 / WIN, -(WIN // 2) / WIN)
            then(V.scalar_tensor_tensor(win_f[:], lo_f[:], -float(WIN), src_f[:], ALU.mult, ALU.add))
            dve.wait_ge(dst_in, 16)
            then(V.tensor_copy(src_f[:], dst_i[:]))
            then(V.tensor_scalar(src_f[:], src_f[:], float(KEY), 1.0, ALU.mult, ALU.add))
            then(V.tensor_tensor(payload[:, :, 0], src_f[:], lo_f[:], ALU.add))
            dve.wait_ge(w_in_sem, 16)
            then(V.tensor_copy(payload[:, :, 1], w_in[:]))

            def place_edges(k):
                n, c0, c, t0 = LOAD[k], COL0[k], TILES[k], GT * GRP0[k]
                hot3 = in_win[:, 0:WIN * n].rearrange("p (b t) -> p b t", b=WIN)
                place3 = place[:, 0:WIN * n].rearrange("p (b t) -> p b t", b=WIN)
                then(V.tensor_tensor(hot3, win_f[:, c0:c0 + n].unsqueeze(1).to_broadcast([EP, WIN, n]),
                                     iota_f[0:EP, 0:WIN].unsqueeze(2).to_broadcast([EP, WIN, n]), ALU.is_equal))
                then(V.tensor_tensor_scan(count[:, 0:WIN * n], keep[n][:].rearrange("p b t -> p (b t)"),
                                          in_win[:, 0:WIN * n], 0.0, ALU.mult, ALU.add))
                count3 = count[:, 0:WIN * n].rearrange("p (b t) -> p b t", b=WIN)
                V.tensor_copy(small[0:EP, 0, :], count3[:, :, n - 1]).then_inc(totals_ready, 1)
                dve.wait_ge(offsets_ready, k + 1)
                then(V.tensor_copy(small[0:EP, 6, :], sort_ps[0:EP, 0:WIN]))
                then(V.tensor_copy(small[0:EP, 11, :], sort_ps[0:EP, 32:32 + WIN]))
                scaled_round(small[0:WIN, 8, 0:1], small[0:WIN, 7, 0:1], sort_ps[0:WIN, 64:65],
                             1.0 / SLOT, (SLOT / 2 - 0.5) / SLOT)
                V.tensor_copy(small[0:WIN, 10, 0:1], small[0:WIN, 8, 0:1]).then_inc(pads_ready, 1)
                scaled_round(small[0:EP, 2, :], small[0:EP, 1, :], small[0:EP, 11, :],
                             1.0 / SLOT, (SLOT / 2 - 0.5) / SLOT)
                then(V.tensor_tensor_scan(small[0:EP, 3, :], ones[0:EP, 0:WIN], small[0:EP, 2, :], 0.0,
                                          ALU.mult, ALU.add))
                then(V.tensor_tensor(small[0:EP, 4, :], small[0:EP, 3, :], small[0:EP, 2, :], ALU.subtract))
                then(V.scalar_tensor_tensor(small[0:EP, 5, :], small[0:EP, 4, :], float(SLOT),
                                            small[0:EP, 6, :], ALU.mult, ALU.add))
                dve.wait_ge(ends_ready, k + 1)
                then(V.tensor_copy(small[0:WIN, 9, 0:1], sort_ps[0:WIN, 96:97]))
                V.tensor_scalar(ge[0:WIN - 1, 0:c], iota_f[0:WIN - 1, 0:c], small[0:WIN - 1, 9, 0:1], None,
                                ALU.is_ge).then_inc(ge_ready, 1)
                then(V.tensor_tensor(place3, count3, small[0:EP, 5, :].unsqueeze(2).to_broadcast([EP, WIN, n]), ALU.add))
                then(V.tensor_tensor(place3, place3, hot3, ALU.mult))
                then(V.tensor_reduce(slot[:, 0:n], place3.rearrange("p b t -> p t b"), AX.X, ALU.add))
                scaled_round(col_s[:, 0:n], slot_t[:, 0:n], slot[:, 0:n], 1.0 / SLOT, -(SLOT / 2 + 0.5) / SLOT)
                then(V.scalar_tensor_tensor(row_s[:, 0:n], col_s[:, 0:n], -float(SLOT), slot[:, 0:n], ALU.mult, ALU.add))
                dve.wait_ge(window_ready, k + 1)
                then(V.tensor_scalar(p_at[0:1, t0:t0 + c], sort_ps[0:1, 128:128 + c], float(SPLITS * HID), None, ALU.mult))
                V.tensor_scalar(agg_at[0:1, t0:t0 + c], sort_ps[0:1, 128:128 + c], float(LO), None,
                                ALU.mult).then_inc(slots_ready, 1)
                dve.wait_ge(slots_ready, k + 1)

            def sort_tile(k, j, b, late):
                c = TILES[k]
                if late:
                    dve.wait_ge(sort_mm, j + (COL0[k] - 3))
                at = (lambda t, i: t[:, i:i + 1]) if isinstance(j, int) else (lambda t, i: t[:, bass.ds(i, 1)])
                V.tensor_scalar(row_hot[:, b, :], iota1_f[0:EP, :], at(row_s, j), None,
                                ALU.is_equal).then_inc(hots_ready, 1)
                pay = (payload[:, COL0[k] + j, :] if isinstance(j, int)
                       else payload[:].rearrange("p t v -> p (t v)")[:, bass.ds(j * 2 + 2 * COL0[k], 2)])
                V.scalar_tensor_tensor(col_hot[:, b, :, 0:c],
                                       iota_f[0:EP, 0:c].unsqueeze(1).to_broadcast([EP, 2, c]), at(col_s, j),
                                       pay.unsqueeze(2).to_broadcast([EP, 2, c]),
                                       ALU.is_equal, ALU.mult).then_inc(hots_ready, 1)

            def read_sorted(k):
                c, t0 = TILES[k], GT * GRP0[k]
                dve.wait_ge(sorted_ready, k + 1)
                then(V.tensor_copy(key_s[:, 0:c], sort_ps[:, 0:c]))
                then(V.tensor_copy(w_s[:, 0, 0:c], sort_ps[:, c:2 * c]))
                scaled_round(dst_f[:, 0:c], slot_k[:, 0:c], key_s[:, 0:c], 1.0 / KEY, -(KEY / 2 - 0.5) / KEY)
                then(V.tensor_copy(q_index[:, t0:t0 + c], dst_f[:, 0:c]))
                then(V.scalar_tensor_tensor(lo1[:, t0:t0 + c], dst_f[:, 0:c], -float(KEY), key_s[:, 0:c], ALU.mult, ALU.add))
                for s in range(SPLITS - 1):
                    then(V.tensor_copy(w_parts[:, t0:t0 + c, s], w_s[:, s, 0:c]))
                    then(V.tensor_tensor(w_s[:, s + 1, 0:c], w_s[:, s, 0:c], w_parts[:, t0:t0 + c, s], ALU.subtract))
                V.tensor_copy(w_parts[:, t0:t0 + c, SPLITS - 1], w_s[:, SPLITS - 1, 0:c]).then_inc(tables_ready, 1)
                dve.wait_ge(tables_ready, k + 1)

            def one_hots(g, u, n):
                if n >= 2:
                    dve.wait_ge(hotT_ps_ready, g - 1)
                    dve.wait_ge(hot32_ready, g - 1)
                if isinstance(g, int):
                    lo_g, w_g = lo1[:, GT * g:GT * g + GT], w_parts[:, GT * g:GT * g + GT, :]
                else:
                    lo_g = lo1[:, bass.ds(g * GT, GT)]
                    w_g = w_parts[:].rearrange("p t s -> p (t s)")[:, bass.ds(g * (GT * SPLITS), GT * SPLITS)] \
                        .rearrange("p (t s) -> p t s", s=SPLITS)
                V.tensor_tensor(hot[:, u % 2, :, 0:LO], lo_plus1[:].unsqueeze(1).to_broadcast([128, GT, LO]),
                                lo_g.unsqueeze(2).to_broadcast([128, GT, LO]), ALU.is_equal).then_inc(hot_ready, 1)
                V.tensor_copy(hot[:, u % 2, :, LO:128], w_g).then_inc(hot_ready, 1)

            def add_segments(m):
                at = agg_at[0:1, GT * m:GT * m + GT] if isinstance(m, int) else agg_at[0:1, bass.ds(m * GT, GT)]
                windows = nc.values_load_multi_w_load_instructions(
                    at, engines=(ENG.DVE,), min_val=0, max_val=(WIN - 1) * LO,
                    skip_runtime_bounds_check_because="a window's number is a count of 24 comparisons")[1]
                dve.wait_ge(seg_ready, m + 1)
                for j in range(GT):
                    dve.wait_ge(agg_added, m * GT + (j + 1))
                    o = agg[j % 2][:, bass.ds(windows[j], LO)]
                    V.tensor_tensor(o, o, seg_ps[:, j * LO:(j + 1) * LO], ALU.add).then_inc(agg_added, 1)

            def step(g, u, n, k=None, j0=None):
                one_hots(g, u, n)
                if k is not None:
                    for i in range(SORTS):
                        sort_tile(k, j0 + i, (SORTS * u + i) % 4, n == LATE or SORTS * u + i >= 4)
                if n >= 4:
                    add_segments(g - 4)

            dve.wait_ge(fills_ready, FILLS)
            place_edges(0)
            for j in range(4):
                sort_tile(0, j, j, False)
            with dve.Fori(4, (LOAD[0] - 1) // 4 * 4 - (4 - 1), 4) as j:
                for b in range(4):
                    sort_tile(0, j + b, b, True)
            for j in range((LOAD[0] - 1) // 4 * 4, LOAD[0]):
                sort_tile(0, j, j % 4, True)
            dve.wait_ge(w_loaded, 16 * W_LOADS)
            then(V.tensor_copy(res_sb[0:NF, :], ident_f[0:NF, 0:NF]))
            for s in range(SPLITS):
                left = b2_in[:] if s == 0 else b2_work[:, 1, :]
                then(V.tensor_copy(b2_part[:], left))
                then(V.tensor_tensor(b2_work[:, 1, :], left, b2_part[:], ALU.subtract))
                if s == 0:
                    then(V.tensor_scalar(b2_work[:, 0, :], b2_part[:], ident_f[0:SPLITS, 0:1], None, ALU.mult))
                else:
                    then(V.scalar_tensor_tensor(b2_work[:, 0, :], b2_part[:], ident_f[0:SPLITS, s:s + 1],
                                                b2_work[:, 0, :], ALU.mult, ALU.add))
            V.tensor_copy(b2_rows[0:SPLITS], b2_work[:, 0, :].unsqueeze(1).to_broadcast([SPLITS, GT, HID])) \
                .then_inc(b2_ready, 1)
            read_sorted(0)
            place_edges(1)
            for k in range(CHUNKS):
                g0, g1 = GRP0[k], GRP0[k] + TILES[k] // GT
                mixed = g0 + (LOAD[k + 1] // SORTS if k + 1 < CHUNKS else 0)
                if k == 0:
                    for u in range(UNROLL):
                        step(u, u, u, 1, SORTS * u)
                elif mixed > g0:
                    for u in range(UNROLL):
                        step(g0 + u, u, 98, k + 1, SORTS * u)
                if mixed > g0:
                    with dve.Fori(g0 + UNROLL, mixed - (UNROLL - 1), UNROLL) as g:
                        for u in range(UNROLL):
                            step(g + u, u, LATE, k + 1, g * SORTS + SORTS * (u - g0))
                    read_sorted(k + 1)
                if k + 2 < CHUNKS:
                    place_edges(k + 2)
                if g1 > mixed:
                    with dve.Fori(mixed, g1 - (UNROLL - 1), UNROLL) as g:
                        for u in range(UNROLL):
                            step(g + u, u, LATE)
            for m in range(GROUPS - 4, GROUPS):
                add_segments(m)

            dve.wait_ge(agg_added, GT * GROUPS + 2)
            for b0, b1 in xt_spans:
                a = agg[0][:, b0 * LO:b1 * LO]
                V.tensor_tensor(a, a, agg[1][:, b0 * LO:b1 * LO], ALU.add).then_inc(agg_whole, 1)
            for n, (b0, b1) in enumerate(ln_spans):
                w = b1 - b0
                y3 = y_banks[n % 2][0:LO, 0:w * NF].rearrange("p (b f) -> p b f", b=w)
                dve.wait_ge(y_ready, n + 1)
                then(V.tensor_reduce(stat[:, 3, b0:b1], y3, AX.X, ALU.add))
                then(V.tensor_scalar(stat[:, 0, b0:b1], stat[:, 3, b0:b1], 1.0 / NF, None, ALU.mult))
                V.tensor_tensor(seg(yc, b0, b1), y3, stat[:, 0, b0:b1].unsqueeze(2).to_broadcast([LO, w, NF]),
                                ALU.subtract).then_inc(y_read, 1)
                dve.wait_ge(y_read, n + 1)
                then(V.tensor_tensor(seg(sq, b0, b1), seg(yc, b0, b1), seg(yc, b0, b1), ALU.mult))
                then(V.tensor_reduce(stat[:, 3, b0:b1], seg(sq, b0, b1), AX.X, ALU.add))
            V.tensor_scalar(stat[:, 1, :], stat[:, 3, :], 1.0 / NF, EPS, ALU.mult, ALU.add).then_inc(ln_var, 1)
            dve.wait_ge(ln_sd, 1)
            then(V.reciprocal(stat[:, 0, :], stat[:, 2, :]))
            for b0, b1 in ln_spans:
                V.tensor_tensor(seg(yc, b0, b1), seg(yc, b0, b1),
                                stat[:, 0, b0:b1].unsqueeze(2).to_broadcast([LO, b1 - b0, NF]),
                                ALU.mult).then_inc(ln_done, 1)


_INS = ["x", "src", "dst", "edge_weight1", "L0_gnn_eW1", "L0_gnn_eb1", "L0_gnn_eW2", "L0_gnn_eb2",
        "L0_gnn_nW1", "L0_gnn_nb1", "L0_gnn_nW2", "L0_gnn_nb2"]


def kernel(**inputs):
    import numpy as _np
    import concourse.bacc as _bacc
    from concourse import mybir as _mybir
    from concourse.bass_utils import run_bass_kernel_spmd as _run

    nc = _bacc.Bacc("TRN2", target_bir_lowering=False, num_devices=1)
    arrays, args = {}, []
    for name in _INS:
        a = _np.ascontiguousarray(inputs[name])
        arrays[f"in_{name}_dram"] = a
        args.append(nc.dram_tensor(f"in_{name}_dram", a.shape, _mybir.dt.from_np(a.dtype), kind="ExternalInput").ap())
    args.append(nc.dram_tensor("out_0_dram", (NODES, NF), _mybir.dt.float32, kind="ExternalOutput").ap())
    build(nc, *args)
    r = _run(nc, [arrays], core_ids=[0])
    return r.results[0]["out_0_dram"]
```

```python
from contextlib import ExitStack

import concourse.bass as bass
from concourse import mybir

F32 = mybir.dt.float32
F16 = mybir.dt.float16
BF16 = mybir.dt.bfloat16
I32 = mybir.dt.int32
ALU = mybir.AluOpType
ACT = mybir.ActivationFunctionType
AX = mybir.AxisListType
ENG = mybir.EngineType

NODES, NF, HID = 3125, 64, 128
EDGES = 53125
LO = 125
WIN = NODES // LO
EP = 125
ECOL = EDGES // EP
SLOT = 128
GT = 4
UNROLL = 4
LOAD = [65, 120, 120, 120]
BATCH = [5, 6, 6, 6]
EPS = 1e-5
ROUND = 1.5 * 2.0 ** 23
KEY = 128
SPLITS = 3


def sorted_tiles(cols):
    worst = (EP * cols + WIN * (SLOT - 1)) // SLOT
    step = GT * UNROLL
    return -(-worst // step) * step


TILES = [sorted_tiles(s) for s in LOAD]
CHUNKS = len(LOAD)
COL0 = [sum(LOAD[:k]) for k in range(CHUNKS)]
GRP0 = [sum(TILES[:k]) // GT for k in range(CHUNKS)]
ALL_TILES = sum(TILES)
GROUPS = ALL_TILES // GT
CMAX, SMAX, BMAX = max(TILES), max(LOAD), max(BATCH)
BAT0 = [sum(n // b for n, b in zip(LOAD[:k], BATCH)) for k in range(CHUNKS)]
MIXED = [n // b for n, b in zip(LOAD, BATCH)]
PLACES = 12
COUNTS, SUMS = 5, 4
assert SMAX <= 2 * NF and sum(LOAD) == ECOL and EP * ECOL == EDGES and LO * WIN == NODES
assert all(n % b == 0 for n, b in zip(LOAD, BATCH)) and 3 * CMAX <= 512 and WIN % COUNTS == 0
assert UNROLL + MIXED[1] == TILES[0] // GT and all(
    MIXED[k + 1] % UNROLL == 0 and MIXED[k + 1] + PLACES + UNROLL <= TILES[k] // GT for k in range(1, CHUNKS - 1))

XT_W = 4
LN_W = 5


LATE = 99


def spans(n, step):
    return [(a, min(a + step, n)) for a in range(0, n, step)]


def build(nc, x, src, dst, edge_weight, eW1, eb1, eW2, eb2, nW1, nb1, nW2, nb2, out):
    with ExitStack() as ctx:
        def sb(name, shape, dt=F32):
            return ctx.enter_context(nc.sbuf_tensor(name, shape, dt))

        def ps(name, shape, dt=F32):
            return ctx.enter_context(nc.psum_tensor(name, shape, dt))

        def sem(name):
            return ctx.enter_context(nc.semaphore(name))

        q_table = nc.dram_tensor("q_table", [NODES, HID], F32).ap()

        iota_i = sb("iota_i", [128, CMAX], I32)
        part_i = sb("part_i", [128, 1], I32)
        iota_f = sb("iota_f", [128, CMAX])
        iota0_b = sb("iota0_b", [128, CMAX], BF16)
        iota1_b = sb("iota1_b", [128, 128], BF16)
        part_f = sb("part_f", [128, 1])
        ident_f = sb("ident_f", [128, 128])
        ident_b = sb("ident_b", [128, 128], BF16)
        before = sb("before", [128, 128])
        upto = sb("upto", [WIN, WIN])
        ones = sb("ones", [128, 128])
        zeros = sb("zeros", [128, 512])
        ones3 = sb("ones3", [128, 128], BF16)
        keep = {n: sb(f"keep{n}", [EP, WIN, n], BF16) for n in sorted(set(LOAD))}
        w1_sb = sb("w1_sb", [NF + 1, 2 * HID])
        w2_sb = sb("w2_sb", [HID, HID])
        b2_in = sb("b2_in", [SPLITS, HID])
        b2_part = sb("b2_part", [SPLITS, HID], BF16)
        b2_work = sb("b2_work", [SPLITS, 2, HID])
        b2_rows = sb("b2_rows", [128, GT, HID], BF16)
        n1x_sb = sb("n1x_sb", [NF, HID])
        n1a_sb = sb("n1a_sb", [HID, HID])
        nb1_sb = sb("nb1_sb", [HID, 1])
        n2_sb = sb("n2_sb", [HID, NF])
        res_sb = sb("res_sb", [NF + 1, NF])
        wc_in = sb("wc_in", [128, HID])
        wc_part = sb("wc_part", [128, SPLITS, HID], BF16)
        wc_rest = sb("wc_rest", [128, SPLITS, HID])
        x_sb = sb("x_sb", [LO, WIN * NF])
        xT = sb("xT", [NF + 1, NODES])
        pq = sb("pq", [128, WIN * 2 * HID])
        p_table = sb("p_table", [128, WIN, SPLITS, HID], BF16)
        sums = [sb(f"sums{i}", [HID, WIN * HID]) for i in range(2)]
        agg = [t[:, 0:NODES] for t in sums]
        rest = sums[1][0:LO, :]
        src_i = sb("src_i", [EP, ECOL], I32)
        dst_i = sb("dst_i", [EP, ECOL], I32)
        w_in = sb("w_in", [EP, ECOL])
        src_f = sb("src_f", [EP, ECOL])
        lo_f = sb("lo_f", [EP, ECOL])
        win_f = sb("win_f", [EP, ECOL])
        work_e = sb("work_e", [EP, 2, ECOL])
        key_in = sb("key_in", [EP, ECOL, 2, 2], F16)
        weight_in = sb("weight_in", [EP, ECOL, SPLITS, 2], BF16)
        in_win = sb("in_win", [EP, WIN * SMAX], BF16)
        count = sb("count", [EP, WIN * SMAX], BF16)
        scratch = sb("scratch", [EP, 2 * WIN * NF])
        place = scratch
        slot = sb("slot", [EP, SMAX])
        slot_t = sb("slot_t", [EP, SMAX])
        col_s = sb("col_s", [EP, SMAX])
        col2 = sb("col2", [EP, SMAX, 2], BF16)
        row2 = sb("row2", [EP, SMAX, 2], BF16)
        small = sb("small", [128, 12, WIN])
        ge = sb("ge", [WIN, CMAX])
        row_hot = sb("row_hot", [EP, 2, BMAX, SLOT], BF16)
        col_hot = sb("col_hot", [EP, 2, BMAX, CMAX], BF16)
        key_hot = sb("key_hot", [EP, 2, BMAX, 2, CMAX], F16)
        weight_hot = sb("weight_hot", [EP, 2, BMAX, SPLITS, CMAX], BF16)
        odd = sb("odd", [128, CMAX])
        turn = sb("turn", [1, ALL_TILES])
        key_s = sb("key_s", [128, 2, CMAX])
        lo2 = sb("lo2", [128, ALL_TILES, 2], BF16)
        w_parts = sb("w_parts", [128, ALL_TILES, SPLITS], BF16)
        q_index = sb("q_index", [128, ALL_TILES])
        rows_at = sb("rows_at", [128, 4, GT], I32)
        p_at = sb("p_at", [1, ALL_TILES], I32)
        agg_at = sb("agg_at", [1, ALL_TILES], I32)
        h1 = pq[:, 2048:3072].rearrange("p (g e) -> p g e", g=2)
        e2 = pq[:, 3072:4096].rearrange("p (g e) -> p g e", g=2)
        q_rows = pq[:, 4096:6144].rearrange("p (g j f) -> p g j f", g=4, j=GT)
        hot = sb("hot", [128, 2, GT, 128], BF16)
        hot32 = pq[:, 0:4 * GT * LO].rearrange("p (g j f) -> p g j f", g=4, j=GT)
        hotT = sb("hotT", [128, 2, GT * 128], BF16)
        hT = pq
        yc = scratch[:, 0:WIN * NF].rearrange("p (b f) -> p b f", b=WIN)
        sq = scratch[:, WIN * NF:2 * WIN * NF].rearrange("p (b f) -> p b f", b=WIN)
        stat = sb("stat", [LO, 4, WIN])

        sort_ps = ps("sort_ps", [128, 512])
        weight_ps = ps("weight_ps", [128, 512])
        hotT_ps = ps("hotT_ps", [128, GT * 128], BF16)
        pre_ps = [ps(f"pre_ps{i}", [128, 512]) for i in range(2)]
        e_ps = [ps(f"e_ps{i}", [128, 512]) for i in range(2)]
        seg_ps = ps("seg_ps", [128, 512])
        y_banks = [sort_ps, seg_ps]
        work_ps = [pre_ps[0], pre_ps[1], e_ps[0], e_ps[1]]

        src_in, dst_in, w_in_sem, x_in, w_loaded, wc_loaded = (
            sem(n) for n in ("src_in", "dst_in", "w_in_sem", "x_in", "w_loaded", "wc_loaded"))
        iotas_ready = sem("iotas_ready")
        fills_ready = sem("fills_ready")
        v_done = sem("v_done")
        s_done = sem("s_done")
        ident_ready = sem("ident_ready")
        xT_ps_ready = sem("xT_ps_ready")
        xT_copied = sem("xT_copied")
        pq_ps_ready = sem("pq_ps_ready")
        pq_copied = sem("pq_copied")
        wc_step = sem("wc_step")
        wc_placed = sem("wc_placed")
        p_part = sem("p_part")
        p_rest = sem("p_rest")
        q_stored = sem("q_stored")
        b2_ready = sem("b2_ready")
        totals_ready = sem("totals_ready")
        offsets_ready = sem("offsets_ready")
        pads_ready = sem("pads_ready")
        ends_ready = sem("ends_ready")
        ge_ready = sem("ge_ready")
        window_ready = sem("window_ready")
        slots_ready = sem("slots_ready")
        cols_ready = sem("cols_ready")
        hots_ready = sem("hots_ready")
        sort_mm = sem("sort_mm")
        sorted_ready = sem("sorted_ready")
        tables_ready = sem("tables_ready")
        rows_in = [sem(f"rows_in{i}") for i in range(4)]
        staged = sem("staged")
        hot_ready = sem("hot_ready")
        hotT_ps_ready = sem("hotT_ps_ready")
        hot32_ready = sem("hot32_ready")
        hotT_ready = sem("hotT_ready")
        pre_ready = sem("pre_ready")
        h1_ready = sem("h1_ready")
        e_ready = sem("e_ready")
        e2_ready = sem("e2_ready")
        seg_ready = sem("seg_ready")
        agg_clear = sem("agg_clear")
        agg_added = sem("agg_added")
        agg_whole = sem("agg_whole")
        hid_ps_ready = sem("hid_ps_ready")
        hid_ready = sem("hid_ready")
        y_ready = sem("y_ready")
        y_read = sem("y_read")
        ln_var = sem("ln_var")
        ln_sd = sem("ln_sd")
        ln_done = sem("ln_done")
        out_stored = sem("out_stored")

        HOTS = 1 + 2 + SPLITS

        xt_spans, ln_spans = spans(WIN, XT_W), spans(WIN, LN_W)
        pq_spans = spans(WIN, 2)

        def seg(ap3, b0, b1):
            return ap3[:, b0:b1, :]

        FILLS = 7 + 2 * len(keep)

        block = ctx.enter_context(nc.Block())

        @block.sync
        def _(sp):
            sp.dma_start(src_i[:], src.rearrange("(p t) -> p t", p=EP)).then_inc(src_in, 16)
            sp.dma_start(dst_i[:], dst.rearrange("(p t) -> p t", p=EP)).then_inc(dst_in, 16)
            sp.dma_start(w_in[:], edge_weight.rearrange("(p t) o -> p (t o)", p=EP)).then_inc(w_in_sem, 16)
            sp.wait_ge(pq_copied, len(pq_spans))
            sp.dma_start(q_table.rearrange("(p b) f -> p b f", b=WIN),
                         pq[0:LO, :].rearrange("p (b h) -> p b h", b=WIN)[:, :, HID:2 * HID]).then_inc(q_stored, 16)
            for n, (b0, b1) in enumerate(ln_spans):
                sp.wait_ge(ln_done, n + 1)
                sp.dma_start(out.rearrange("(p b) f -> p b f", b=WIN)[:, b0:b1, :],
                             seg(yc, b0, b1)).then_inc(out_stored, 16)
            sp.wait_ge(out_stored, 16 * len(ln_spans))

        W_LOADS = 10

        @block.scalar
        def _(act):
            act.dma_start(x_sb[:], x.rearrange("(p b) f -> p (b f)", b=WIN)).then_inc(x_in, 16)
            act.dma_start(w1_sb[0:NF, 0:HID], eW1[0:NF, :]).then_inc(w_loaded, 16)
            act.dma_start(w1_sb[0:NF, HID:2 * HID], eW1[NF:2 * NF, :]).then_inc(w_loaded, 16)
            act.dma_start(w1_sb[NF:NF + 1, 0:HID], eb1.rearrange("(a f) -> a f", a=1)).then_inc(w_loaded, 16)
            act.dma_start(wc_in[96:128, :], eW1[2 * NF:2 * NF + 1, :].to_broadcast([32, HID])).then_inc(wc_loaded, 16)
            act.dma_start(b2_in[:], eb2.rearrange("(a f) -> a f", a=1).to_broadcast([SPLITS, HID])).then_inc(w_loaded, 16)
            act.dma_start(w2_sb[:], eW2).then_inc(w_loaded, 16)
            act.dma_start(n1x_sb[:], nW1[0:NF, :]).then_inc(w_loaded, 16)
            act.dma_start(n1a_sb[:], nW1[NF:NF + HID, :]).then_inc(w_loaded, 16)
            act.dma_start(nb1_sb[:], nb1.rearrange("(f a) -> f a", a=1)).then_inc(w_loaded, 16)
            act.dma_start(n2_sb[:], nW2).then_inc(w_loaded, 16)
            act.dma_start(res_sb[NF:NF + 1, :], nb2.rearrange("(a f) -> a f", a=1)).then_inc(w_loaded, 16)

            for n, (b0, b1) in enumerate(xt_spans):
                act.wait_ge(xT_ps_ready, n + 1)
                nc.scalar.activation(xT[0:NF, b0 * LO:b1 * LO], work_ps[n % 4][0:NF, 0:(b1 - b0) * LO],
                                     ACT.Copy).then_inc(xT_copied, 1)
            for n, (b0, b1) in enumerate(pq_spans):
                act.wait_ge(pq_ps_ready, n + 1)
                nc.scalar.activation(pq[0:LO, b0 * 2 * HID:b1 * 2 * HID],
                                     work_ps[n % 4][0:LO, 0:(b1 - b0) * 2 * HID], ACT.Copy).then_inc(pq_copied, 1)

            act.wait_ge(wc_placed, SPLITS)
            act.wait_ge(pq_copied, len(pq_spans))
            for s in range(SPLITS):
                if s == 0:
                    left = pq[0:LO, :].rearrange("p (b h) -> p b h", b=WIN)[:, :, 0:HID]
                else:
                    act.wait_ge(p_rest, s)
                    left = rest.rearrange("p (b h) -> p b h", b=WIN)
                nc.scalar.activation(p_table[0:LO, :, s, :], left, ACT.Copy).then_inc(p_part, 1)

            def convert(g, u, n):
                act.wait_ge(hot_ready, 2 * g + 2)
                if n >= 4:
                    act.wait_ge(seg_ready, g - 3)
                nc.scalar.activation(hot32[:, u % 4], hot[:, u % 2, :, 0:LO], ACT.Copy).then_inc(hot32_ready, 1)

            def turned(g, u, n):
                act.wait_ge(hotT_ps_ready, g + 1)
                if n >= 2:
                    act.wait_ge(pre_ready, g - 1)
                nc.scalar.activation(hotT[:, u % 2, :], hotT_ps[:], ACT.Copy).then_inc(hotT_ready, 1)

            def silu1(m, u, n):
                act.wait_ge(pre_ready, m + 1)
                if n >= 3:
                    act.wait_ge(e_ready, m - 1)
                nc.scalar.activation(h1[:, u % 2, :], pre_ps[u % 2][:], ACT.Silu).then_inc(h1_ready, 1)

            def silu2(m, u, n):
                act.wait_ge(e_ready, m + 1)
                if n >= 4:
                    act.wait_ge(seg_ready, m - 1)
                nc.scalar.activation(e2[:, u % 2, :], e_ps[u % 2][:], ACT.Silu).then_inc(e2_ready, 1)

            def stage(g, u, n):
                if n >= 4:
                    act.wait_ge(pre_ready, g - 3)
                at = q_index[:, GT * g:GT * g + GT] if isinstance(g, int) else q_index[:, bass.ds(g * GT, GT)]
                nc.scalar.activation(rows_at[:, u % 4, :], at, ACT.Copy).then_inc(staged, 1)

            def step(g, u, n, staging=True):
                convert(g, u, n)
                turned(g, u, n)
                if n >= 1:
                    silu1(g - 1, u + 3, n)
                if staging:
                    stage(g + 3, u + 3, n + 3)
                if n >= 2:
                    silu2(g - 2, u + 2, n)

            act.wait_ge(q_stored, 16)
            act.wait_ge(tables_ready, 1)
            for g in range(3):
                stage(g, g, g)
            for g in range(UNROLL):
                step(g, g, g)
            for k in range(CHUNKS):
                a, b = GRP0[k] + UNROLL * (k == 0) - UNROLL * (k > 1), GRP0[k] + TILES[k] // GT - UNROLL
                if k > 1:
                    act.wait_ge(tables_ready, k + 1)
                with act.Fori(a, b - (UNROLL - 1), UNROLL) as g:
                    for u in range(UNROLL):
                        step(g + u, u, LATE)
                if k == 0:
                    for u in range(UNROLL):
                        step(b + u, u, LATE, u == 0)
                    act.wait_ge(tables_ready, 2)
                    for u in range(3):
                        stage(GRP0[1] + u, u, LATE)
            for u in range(UNROLL):
                step(GROUPS - UNROLL + u, u, LATE, u == 0)
            silu1(GROUPS - 1, UNROLL + 3, LATE)
            silu2(GROUPS - 2, UNROLL + 2, LATE)
            silu2(GROUPS - 1, UNROLL + 3, LATE)

            for n, (b0, b1) in enumerate(xt_spans):
                act.wait_ge(hid_ps_ready, n + 1)
                nc.scalar.activation(hT[:, b0 * LO:b1 * LO], work_ps[n % 4][:, 0:(b1 - b0) * LO], ACT.Silu,
                                     bias=nb1_sb[:, 0:1]).then_inc(hid_ready, 1)
            act.wait_ge(ln_var, 1)
            nc.scalar.activation(stat[:, 2, :], stat[:, 1, :], ACT.Sqrt).then_inc(ln_sd, 1)

        @block.gpsimd
        def _(pool):
            nc.gpsimd.iota(part_i[:], pattern=[[0, 1]], base=0, channel_multiplier=1).then_inc(iotas_ready, 1)
            nc.gpsimd.iota(iota_i[:], pattern=[[1, CMAX]], base=0, channel_multiplier=0).then_inc(iotas_ready, 1)
            fills = ([(ones[:], 1.0)] + [(t[:], 1.0) for t in keep.values()] + [(ones3[:], 0.0), (zeros[:], 0.0),
                     (b2_rows[:], 0.0), (w1_sb[NF:NF + 1, HID:2 * HID], 0.0), (xT[NF:NF + 1, :], 1.0),
                     (ones3[0:SPLITS, :], 1.0)] + [(t[:, :, 0:1], 0.0) for t in keep.values()])
            for n, (t, value) in enumerate(fills):
                pool.wait_ge(fills_ready, n)
                nc.gpsimd.memset(t, value).then_inc(fills_ready, 1)
            pool.wait_ge(fills_ready, FILLS)
            nc.gpsimd.memset(agg[0], 0.0).then_inc(agg_clear, 1)

            pool.wait_ge(wc_loaded, 16)
            pool.wait_ge(agg_clear, 1)
            for s in range(SPLITS):
                left = wc_in[96:128, :] if s == 0 else wc_rest[96:128, s - 1, :]
                nc.gpsimd.tensor_copy(wc_part[96:128, s, :], left).then_inc(wc_step, 1)
                pool.wait_ge(wc_step, 2 * s + 1)
                nc.gpsimd.tensor_tensor(wc_rest[96:128, s, :], left, wc_part[96:128, s, :], ALU.subtract).then_inc(wc_step, 1)
                pool.wait_ge(wc_step, 2 * s + 2)
                nc.gpsimd.tensor_copy(p_table[96:128, :, s, :],
                                      wc_part[96:128, s, :].unsqueeze(1).to_broadcast([32, WIN, HID])).then_inc(wc_placed, 1)
                pool.wait_ge(wc_placed, s + 1)

            for s in range(SPLITS - 1):
                pool.wait_ge(p_part, s + 1)
                left = (pq[0:LO, :].rearrange("p (b h) -> p b h", b=WIN)[:, :, 0:HID] if s == 0
                        else rest.rearrange("p (b h) -> p b h", b=WIN))
                nc.gpsimd.tensor_tensor(rest.rearrange("p (b h) -> p b h", b=WIN), left,
                                        p_table[0:LO, :, s, :], ALU.subtract).then_inc(p_rest, 1)

            pool.wait_ge(p_part, SPLITS)
            nc.gpsimd.memset(agg[1], 0.0).then_inc(agg_added, 2)

            def gather(g, u):
                pool.wait_ge(staged, g + 2)
                nc.gpsimd.tensor_copy(turn[:, bass.ds(g * GT, 1)], q_index[0:1, bass.ds(g * GT, 1)])
                for v in (u, u + 1):
                    for j in range(GT):
                        nc.gpsimd.indirect_dma_start(
                            q_rows[:, v, j, :], None, q_table,
                            bass.IndirectOffsetOnAxis(ap=rows_at[:, v, j:j + 1], axis=0)).then_inc(rows_in[v], 16)

            pool.wait_ge(q_stored, 16)
            with pool.Fori(0, GROUPS - (UNROLL - 1), UNROLL) as g:
                for u in range(0, UNROLL, 2):
                    gather(g + u, u)

        @block.tensor
        def _(pe):
            def mm(o, lhsT, rhs, start, stop, **kw):
                return nc.tensor.matmul(o, lhsT, rhs, start=start, stop=stop, **kw)

            def place_part(k, i):
                if i == COUNTS:
                    pe.wait_ge(totals_ready, k + 1)
                    tot = small[0:EP, 0, :]
                    mm(sort_ps[0:EP, 0:WIN], before[0:EP, 0:EP], tot, True, True)
                    mm(sort_ps[0:EP, 32:32 + WIN], ones[0:EP, 0:EP], tot, True, True)
                    mm(sort_ps[0:WIN, 64:65], tot, ones[0:EP, 0:1], True, True).then_inc(offsets_ready, 1)
                    pe.wait_ge(pads_ready, k + 1)
                    mm(sort_ps[0:WIN, 96:97], upto[:], small[0:WIN, 8, 0:1], True, True).then_inc(ends_ready, 1)
                if i == COUNTS + 1:
                    pe.wait_ge(ge_ready, k + 1)
                    mm(sort_ps[0:1, 128:128 + TILES[k]], ones[0:WIN - 1, 0:1], ge[0:WIN - 1, 0:TILES[k]],
                       True, True).then_inc(window_ready, 1)

            def sort_sums(k, q, b, start, stop):
                c = TILES[k]
                rows = row_hot[:, q, b, :] if b is not None else zeros[0:EP, 0:128]
                keys = key_hot[:, q, b, :, 0:c] if b is not None else zeros[0:EP, 0:2 * c]
                weights = weight_hot[:, q, b, :, 0:c] if b is not None else zeros[0:EP, 0:3 * c]
                mm(sort_ps[:, 0:2 * c], rows, keys, start, stop)
                return mm(weight_ps[:, 0:3 * c], rows, weights, start, stop)

            def sort_open(k):
                pe.wait_ge(slots_ready, k + 1)
                sort_sums(k, 0, None, True, False)

            def sort_batch(k, n, q):
                pe.wait_ge(hots_ready, HOTS * n + HOTS)
                for b in range(BATCH[k]):
                    last = sort_sums(k, q, b, False, False)
                last.then_inc(sort_mm, 1)

            def sort_close(k):
                sort_sums(k, 0, None, False, True).then_inc(sorted_ready, 1)

            pe.wait_ge(x_in, 16)
            pe.wait_ge(ident_ready, 1)
            for n, (b0, b1) in enumerate(xt_spans):
                if n >= 4:
                    pe.wait_ge(xT_copied, n - 3)
                for b in range(b0, b1):
                    last = nc.tensor.transpose(work_ps[n % 4][0:NF, (b - b0) * LO:(b - b0 + 1) * LO],
                                               x_sb[:, b * NF:(b + 1) * NF], ident_f[0:LO, 0:LO])
                last.then_inc(xT_ps_ready, 1)
            pe.wait_ge(xT_copied, len(xt_spans))
            pe.wait_ge(w_loaded, 16 * W_LOADS)
            pe.wait_ge(fills_ready, FILLS)
            for n, (b0, b1) in enumerate(pq_spans):
                if n >= 4:
                    pe.wait_ge(pq_copied, n - 3)
                for b in range(b0, b1):
                    last = mm(work_ps[n % 4][0:LO, (b - b0) * 2 * HID:(b - b0 + 1) * 2 * HID],
                              xT[:, b * LO:(b + 1) * LO], w1_sb[:], True, True)
                last.then_inc(pq_ps_ready, 1)

            for i in range(PLACES):
                place_part(0, i)
            sort_open(0)
            with pe.Fori(0, MIXED[0] - 1 - 1, 2) as n:
                for q in range(2):
                    sort_batch(0, n + q, q)
            sort_batch(0, MIXED[0] - 1, 0)
            sort_close(0)

            def turn(g, u, n):
                pe.wait_ge(hot_ready, 2 * g + 2)
                if n >= 1:
                    pe.wait_ge(hotT_ready, g)
                for j in range(GT):
                    last = nc.tensor.transpose(hotT_ps[:, j * 128:(j + 1) * 128], hot[:, u % 2, j, :], ident_b[:])
                last.then_inc(hotT_ps_ready, 1)

            def tile_windows(m):
                at = p_at[0:1, GT * m:GT * m + GT] if isinstance(m, int) else p_at[0:1, bass.ds(m * GT, GT)]
                return nc.values_load_multi_w_load_instructions(
                    at, engines=(ENG.PE,), min_val=0, max_val=(WIN - 1) * SPLITS * HID,
                    skip_runtime_bounds_check_because="a window's number is a count of 24 comparisons")[1]

            p_flat = p_table[:].rearrange("p b s f -> p (b s f)")

            def first_layer(m, u, n):
                windows = tile_windows(m)
                pe.wait_ge(rows_in[u % 4], rows_count(m, u))
                pe.wait_ge(hotT_ready, m + 1)
                if n >= 3:
                    pe.wait_ge(h1_ready, m - 1)
                for j in range(GT):
                    o = pre_ps[u % 2][:, j * 128:(j + 1) * 128]
                    mm(o, q_rows[:, u % 4, j, :], ident_f[:], True, False, is_transpose=True)
                    for s in range(SPLITS):
                        last = mm(o, p_flat[:, bass.ds(windows[j] + s * HID, HID)],
                                  hotT[:, u % 2, j * 128:(j + 1) * 128], False, s == SPLITS - 1)
                last.then_inc(pre_ready, 1)

            def rows_count(m, u):
                if isinstance(m, int):
                    return 16 * GT * (m // 4 + 1)
                return (m - u % 4) * (16 * GT // 4) + 16 * GT

            def second_layer(m, u, n):
                pe.wait_ge(h1_ready, m + 1)
                if n >= 4:
                    pe.wait_ge(e2_ready, m - 1)
                mm(e_ps[u % 2][:], ones3[:], b2_rows[:].rearrange("p j f -> p (j f)"), True, False)
                for j in range(GT):
                    last = mm(e_ps[u % 2][:, j * HID:(j + 1) * HID], h1[:, u % 2, j * 128:(j + 1) * 128], w2_sb[:],
                              False, j == GT - 1)
                last.then_inc(e_ready, 1)

            def segment(m, u, n):
                pe.wait_ge(e2_ready, m + 1)
                pe.wait_ge(hot32_ready, m + 1)
                if n >= 4:
                    pe.wait_ge(agg_added, m * GT + 2)
                for j in range(GT):
                    last = mm(seg_ps[:, j * LO:(j + 1) * LO], e2[:, u % 2, j * HID:(j + 1) * HID],
                              hot32[:, u % 4, j, :], True, True)
                last.then_inc(seg_ready, 1)

            def step(g, u, n, k=None, batch=None):
                turn(g, u, n)
                if n >= 1:
                    first_layer(g - 1, u + 3, n)
                if k is not None:
                    sort_batch(k, batch, u % 2)
                if n >= 2:
                    second_layer(g - 2, u + 2, n)
                if n >= 3:
                    segment(g - 3, u + 1, n)

            pe.wait_ge(p_part, SPLITS)
            pe.wait_ge(b2_ready, 1)
            pe.wait_ge(tables_ready, 1)
            for u in range(UNROLL):
                for i in range(PLACES // UNROLL * u, PLACES // UNROLL * (u + 1)):
                    place_part(1, i)
                step(u, u, u)
            for k in range(CHUNKS):
                g0, g1 = GRP0[k], GRP0[k] + TILES[k] // GT
                pe.wait_ge(tables_ready, k + 1)
                if k + 1 == CHUNKS:
                    with pe.Fori(g0, g1 - (UNROLL - 1), UNROLL) as g:
                        for u in range(UNROLL):
                            step(g + u, u, LATE)
                    continue
                for i in range(PLACES if k > 0 else 0):
                    place_part(k + 1, i)
                    step(g0 + i, i % UNROLL, LATE)
                g0 += PLACES if k > 0 else UNROLL
                sort_open(k + 1)
                with pe.Fori(g0, g0 + MIXED[k + 1] - (UNROLL - 1), UNROLL) as g:
                    for u in range(UNROLL):
                        step(g + u, u, LATE, k + 1, g + (u + BAT0[k + 1] - g0))
                sort_close(k + 1)
                for g in range(g0 + MIXED[k + 1], g1):
                    step(g, g % UNROLL, LATE)
            u = UNROLL
            first_layer(GROUPS - 1, u + 3, LATE)
            second_layer(GROUPS - 2, u + 2, LATE)
            segment(GROUPS - 3, u + 1, LATE)
            second_layer(GROUPS - 1, u + 3, LATE)
            segment(GROUPS - 2, u + 2, LATE)
            segment(GROUPS - 1, u + 3, LATE)

            for n, (b0, b1) in enumerate(xt_spans):
                o = work_ps[n % 4][:, 0:(b1 - b0) * LO]
                if n >= 4:
                    pe.wait_ge(hid_ready, n - 3)
                else:
                    pe.wait_ge(e2_ready, GROUPS)
                mm(o, n1x_sb[:], xT[0:NF, b0 * LO:b1 * LO], True, False)
                pe.wait_ge(agg_whole, n + 1)
                mm(o, n1a_sb[:], agg[0][:, b0 * LO:b1 * LO], False, True).then_inc(hid_ps_ready, 1)
            for n, (b0, b1) in enumerate(ln_spans):
                pe.wait_ge(hid_ready, -(-b1 // XT_W))
                if n >= len(y_banks):
                    pe.wait_ge(y_read, n - len(y_banks) + 1)
                for b in range(b0, b1):
                    o = y_banks[n % len(y_banks)][0:LO, (b - b0) * NF:(b - b0 + 1) * NF]
                    mm(o, hT[:, b * LO:(b + 1) * LO], n2_sb[:], True, False)
                    last = mm(o, xT[:, b * LO:(b + 1) * LO], res_sb[:], False, True)
                last.then_inc(y_ready, 1)

        @block.vector
        def _(dve):
            V = nc.vector
            steps = [0]

            def then(ins):
                steps[0] += 1
                ins.then_inc(v_done, 1)
                dve.wait_ge(v_done, steps[0])

            def scaled_round(dst, tmp, src, scale, shift):
                then(V.tensor_scalar(tmp, src, scale, shift, ALU.mult, ALU.add))
                then(V.tensor_scalar(dst, tmp, ROUND, -ROUND, ALU.add, ALU.add))

            dve.wait_ge(iotas_ready, 2)
            then(V.tensor_copy(iota_f[:], iota_i[:]))
            then(V.tensor_copy(part_f[:], part_i[:]))
            V.tensor_scalar(ident_f[:], iota_f[:, 0:128], part_f[:, 0:1], None, ALU.is_equal).then_inc(ident_ready, 1)
            dve.wait_ge(ident_ready, 1)
            then(V.tensor_copy(ident_b[:], ident_f[:]))
            then(V.tensor_scalar(before[:], iota_f[:, 0:128], part_f[:, 0:1], None, ALU.is_gt))
            then(V.tensor_scalar(upto[:], iota_f[0:WIN, 0:WIN], part_f[0:WIN, 0:1], None, ALU.is_ge))
            then(V.tensor_scalar(iota1_b[:], iota_f[:, 0:128], 1.0, None, ALU.add))
            then(V.tensor_copy(iota0_b[:], iota_f[:]))

            dve.wait_ge(src_in, 16)
            then(V.tensor_copy(src_f[:], src_i[:]))
            scaled_round(lo_f[:], win_f[:], src_f[:], 1.0 / WIN, -(WIN // 2) / WIN)
            then(V.scalar_tensor_tensor(win_f[:], lo_f[:], -float(WIN), src_f[:], ALU.mult, ALU.add))
            dve.wait_ge(dst_in, 16)
            half, rem = work_e[:, 0, :], work_e[:, 1, :]

            def twice(ap):
                return ap.unsqueeze(2).to_broadcast([EP, ap.shape[1], 2])

            then(V.tensor_copy(src_f[:], dst_i[:]))
            scaled_round(half, rem, src_f[:], 0.5, -0.25)
            then(V.scalar_tensor_tensor(rem, half, -2.0, src_f[:], ALU.mult, ALU.add))
            then(V.tensor_scalar(rem, rem, float(KEY), 1.0, ALU.mult, ALU.add))
            then(V.tensor_tensor(rem, rem, lo_f[:], ALU.add))
            then(V.tensor_copy(key_in[:, :, 0, :], twice(half)))
            then(V.tensor_copy(key_in[:, :, 1, :], twice(rem)))
            dve.wait_ge(w_in_sem, 16)
            left = w_in[:]
            for s in range(SPLITS):
                then(V.tensor_copy(weight_in[:, :, s, :], twice(left)))
                if s < SPLITS - 1:
                    then(V.tensor_tensor(work_e[:, s, :], left, weight_in[:, :, s, 0], ALU.subtract))
                    left = work_e[:, s, :]

            def place_part(k, i):
                n, c0, c, t0 = LOAD[k], COL0[k], TILES[k], GT * GRP0[k]
                win3, count3, place3 = (t[:, 0:WIN * n].rearrange("p (b t) -> p b t", b=WIN)
                                        for t in (in_win, count, place))
                if i < COUNTS:
                    b0, b1 = WIN // COUNTS * i, WIN // COUNTS * (i + 1)
                    shape = [EP, b1 - b0, n]
                    then(V.tensor_tensor(win3[:, b0:b1, :], win_f[:, c0:c0 + n].unsqueeze(1).to_broadcast(shape),
                                         iota_f[0:EP, b0:b1].unsqueeze(2).to_broadcast(shape), ALU.is_equal))
                    then(V.tensor_tensor_scan(count[:, b0 * n:b1 * n],
                                              keep[n][:, b0:b1, :].rearrange("p b t -> p (b t)"),
                                              in_win[:, b0 * n:b1 * n], 0.0, ALU.mult, ALU.add))
                    if i == COUNTS - 1:
                        V.tensor_copy(small[0:EP, 0, :], count3[:, :, n - 1]).then_inc(totals_ready, 1)
                elif i == COUNTS:
                    dve.wait_ge(offsets_ready, k + 1)
                    then(V.tensor_copy(small[0:EP, 6, :], sort_ps[0:EP, 0:WIN]))
                    then(V.tensor_copy(small[0:EP, 11, :], sort_ps[0:EP, 32:32 + WIN]))
                    scaled_round(small[0:WIN, 8, 0:1], small[0:WIN, 7, 0:1], sort_ps[0:WIN, 64:65],
                                 1.0 / SLOT, (SLOT / 2 - 0.5) / SLOT)
                    V.tensor_copy(small[0:WIN, 10, 0:1], small[0:WIN, 8, 0:1]).then_inc(pads_ready, 1)
                    scaled_round(small[0:EP, 2, :], small[0:EP, 1, :], small[0:EP, 11, :],
                                 1.0 / SLOT, (SLOT / 2 - 0.5) / SLOT)
                    then(V.tensor_tensor_scan(small[0:EP, 3, :], ones[0:EP, 0:WIN], small[0:EP, 2, :], 0.0,
                                              ALU.mult, ALU.add))
                    then(V.tensor_tensor(small[0:EP, 4, :], small[0:EP, 3, :], small[0:EP, 2, :], ALU.subtract))
                    then(V.scalar_tensor_tensor(small[0:EP, 5, :], small[0:EP, 4, :], float(SLOT),
                                                small[0:EP, 6, :], ALU.mult, ALU.add))
                    dve.wait_ge(ends_ready, k + 1)
                    then(V.tensor_copy(small[0:WIN, 9, 0:1], sort_ps[0:WIN, 96:97]))
                    V.tensor_scalar(ge[0:WIN - 1, 0:c], iota_f[0:WIN - 1, 0:c], small[0:WIN - 1, 9, 0:1], None,
                                    ALU.is_ge).then_inc(ge_ready, 1)
                elif i <= COUNTS + SUMS:
                    step_t = -(-n // SUMS)
                    a, b = step_t * (i - COUNTS - 1), min(step_t * (i - COUNTS), n)
                    shape = [EP, WIN, b - a]
                    p3 = place3[:, :, a:b]
                    then(V.tensor_tensor(p3, count3[:, :, a:b], small[0:EP, 5, :].unsqueeze(2).to_broadcast(shape),
                                         ALU.add))
                    then(V.tensor_tensor(p3, p3, win3[:, :, a:b], ALU.mult))
                    then(V.tensor_reduce(slot[:, a:b], p3.rearrange("p b t -> p t b"), AX.X, ALU.add))
                elif i == COUNTS + SUMS + 1:
                    scaled_round(col_s[:, 0:n], slot_t[:, 0:n], slot[:, 0:n], 1.0 / SLOT, -(SLOT / 2 + 0.5) / SLOT)
                    then(V.tensor_copy(col2[:, 0:n, :], twice(col_s[:, 0:n])))
                    then(V.scalar_tensor_tensor(slot[:, 0:n], col_s[:, 0:n], -float(SLOT), slot[:, 0:n],
                                                ALU.mult, ALU.add))
                    then(V.tensor_copy(row2[:, 0:n, :], twice(slot[:, 0:n])))
                    dve.wait_ge(window_ready, k + 1)
                    then(V.tensor_scalar(p_at[0:1, t0:t0 + c], sort_ps[0:1, 128:128 + c], float(SPLITS * HID),
                                         None, ALU.mult))
                    V.tensor_scalar(agg_at[0:1, t0:t0 + c], sort_ps[0:1, 128:128 + c], float(LO), None,
                                    ALU.mult).then_inc(slots_ready, 1)
                    dve.wait_ge(slots_ready, k + 1)

            def pairs(ap, dims, size):
                return ap.unsqueeze(2).to_broadcast([dims[0], dims[1], size // 2, 2])

            def split2(ap, **kw):
                return ap.rearrange("p v (a b) -> p v a b", b=2)

            def sort_batch(k, n, j, q, late, between=None):
                c, m = TILES[k], BATCH[k]
                if late:
                    dve.wait_ge(sort_mm, n - 1)

                def of(t, start, size, v):
                    if isinstance(start, int):
                        return t[:, start:start + size].rearrange("p t e -> p (t e)")
                    return t[:].rearrange("p t e -> p (t e)")[:, bass.ds(start * v, size * v)]

                def against(t, start, size, v, width):
                    return of(t, start, size, v).rearrange("p (a b) -> p a b", b=2).unsqueeze(2) \
                        .to_broadcast([EP, size * v // 2, width // 2, 2])

                def iota(t, width):
                    return t[0:EP, 0:width].rearrange("p (a b) -> p a b", b=2).unsqueeze(1) \
                        .to_broadcast([EP, m, width // 2, 2])

                V.tensor_tensor(split2(col_hot[:, q, 0:m, 0:c]), iota(iota0_b, c), against(col2, j, m, 2, c),
                                ALU.is_equal).then_inc(cols_ready, 1)
                V.tensor_tensor(split2(row_hot[:, q, 0:m, :]), iota(iota1_b, SLOT), against(row2, j, m, 2, SLOT),
                                ALU.is_equal).then_inc(hots_ready, 1)
                if between is not None:
                    place_weights(*between)
                dve.wait_ge(cols_ready, n + 1)
                cols = split2(col_hot[:, q, 0:m, 0:c])
                for t, payload, values in ((key_hot, key_in2, 2), (weight_hot, weight_in3, SPLITS)):
                    at = of(payload, j + COL0[k], m, 2 * values).rearrange("p (b v e) -> p b v e", b=m, v=values)
                    for v in range(values):
                        V.tensor_tensor(split2(t[:, q, 0:m, v, 0:c]), cols,
                                        at[:, :, v, :].unsqueeze(2).to_broadcast([EP, m, c // 2, 2]),
                                        ALU.mult).then_inc(hots_ready, 1)

            key_in2 = key_in[:].rearrange("p t v e -> p t (v e)")
            weight_in3 = weight_in[:].rearrange("p t v e -> p t (v e)")

            def read_sorted(k):
                c, t0 = TILES[k], GT * GRP0[k]
                dve.wait_ge(sorted_ready, k + 1)
                then(V.tensor_copy(key_s[:, :, 0:c], sort_ps[:, 0:2 * c].rearrange("p (v c) -> p v c", v=2)))
                then(V.tensor_scalar(odd[:, 0:c], key_s[:, 1, 0:c], float(KEY), None, ALU.is_ge))
                then(V.scalar_tensor_tensor(q_index[:, t0:t0 + c], key_s[:, 0, 0:c], 2.0, odd[:, 0:c],
                                            ALU.mult, ALU.add))
                then(V.scalar_tensor_tensor(key_s[:, 1, 0:c], odd[:, 0:c], -float(KEY), key_s[:, 1, 0:c],
                                            ALU.mult, ALU.add))
                then(V.tensor_copy(lo2[:, t0:t0 + c, :], key_s[:, 1, 0:c].unsqueeze(2).to_broadcast([128, c, 2])))
                V.tensor_copy(w_parts[:, t0:t0 + c, :], weight_ps[:, 0:SPLITS * c].rearrange("p (v c) -> p c v", c=c)) \
                    .then_inc(tables_ready, 1)
                dve.wait_ge(tables_ready, k + 1)

            def one_hots(g, u, n):
                if n >= 2:
                    dve.wait_ge(hotT_ps_ready, g - 1)
                    dve.wait_ge(hot32_ready, g - 1)
                if isinstance(g, int):
                    lo_g = lo2[:, GT * g:GT * g + GT, :]
                else:
                    lo_g = lo2[:].rearrange("p t e -> p (t e)")[:, bass.ds(g * (GT * 2), GT * 2)] \
                        .rearrange("p (t e) -> p t e", e=2)
                V.tensor_tensor(split2(hot[:, u % 2]),
                                iota1_b[:].rearrange("p (a b) -> p a b", b=2).unsqueeze(1).to_broadcast([128, GT, 64, 2]),
                                lo_g.unsqueeze(2).to_broadcast([128, GT, 64, 2]), ALU.is_equal).then_inc(hot_ready, 1)

            def place_weights(g, u):
                if isinstance(g, int):
                    w_g = w_parts[:, GT * g:GT * g + GT, :]
                else:
                    w_g = w_parts[:].rearrange("p t s -> p (t s)")[:, bass.ds(g * (GT * SPLITS), GT * SPLITS)] \
                        .rearrange("p (t s) -> p t s", s=SPLITS)
                dve.wait_ge(hot_ready, 2 * g + 1)
                V.tensor_copy(hot[:, u % 2, :, LO:128], w_g).then_inc(hot_ready, 1)

            def add_segments(m):
                at = agg_at[0:1, GT * m:GT * m + GT] if isinstance(m, int) else agg_at[0:1, bass.ds(m * GT, GT)]
                windows = nc.values_load_multi_w_load_instructions(
                    at, engines=(ENG.DVE,), min_val=0, max_val=(WIN - 1) * LO,
                    skip_runtime_bounds_check_because="a window's number is a count of 24 comparisons")[1]
                dve.wait_ge(seg_ready, m + 1)
                for j in range(GT):
                    dve.wait_ge(agg_added, m * GT + (j + 1))
                    o = agg[j % 2][:, bass.ds(windows[j], LO)]
                    V.tensor_tensor(o, o, seg_ps[:, j * LO:(j + 1) * LO], ALU.add).then_inc(agg_added, 1)

            def step(g, u, n, k=None, batch=None, j=None, late=True):
                one_hots(g, u, n)
                if k is not None:
                    sort_batch(k, batch, j, u % 2, late, (g, u))
                else:
                    place_weights(g, u)
                if n >= 4:
                    add_segments(g - 4)

            dve.wait_ge(fills_ready, FILLS)
            for i in range(PLACES):
                place_part(0, i)
            for q in range(2):
                sort_batch(0, q, BATCH[0] * q, q, False)
            with dve.Fori(2, MIXED[0] - 1 - 1, 2) as n:
                for q in range(2):
                    sort_batch(0, n + q, n * BATCH[0] + q * BATCH[0], q, True)
            sort_batch(0, MIXED[0] - 1, LOAD[0] - BATCH[0], 0, True)
            dve.wait_ge(w_loaded, 16 * W_LOADS)
            then(V.tensor_copy(res_sb[0:NF, :], ident_f[0:NF, 0:NF]))
            for s in range(SPLITS):
                left = b2_in[:] if s == 0 else b2_work[:, 1, :]
                then(V.tensor_copy(b2_part[:], left))
                then(V.tensor_tensor(b2_work[:, 1, :], left, b2_part[:], ALU.subtract))
                if s == 0:
                    then(V.tensor_scalar(b2_work[:, 0, :], b2_part[:], ident_f[0:SPLITS, 0:1], None, ALU.mult))
                else:
                    then(V.scalar_tensor_tensor(b2_work[:, 0, :], b2_part[:], ident_f[0:SPLITS, s:s + 1],
                                                b2_work[:, 0, :], ALU.mult, ALU.add))
            V.tensor_copy(b2_rows[0:SPLITS], b2_work[:, 0, :].unsqueeze(1).to_broadcast([SPLITS, GT, HID])) \
                .then_inc(b2_ready, 1)
            read_sorted(0)
            for u in range(UNROLL):
                for i in range(PLACES // UNROLL * u, PLACES // UNROLL * (u + 1)):
                    place_part(1, i)
                step(u, u, u)
            for k in range(CHUNKS):
                g0, g1 = GRP0[k], GRP0[k] + TILES[k] // GT
                if k + 1 == CHUNKS:
                    with dve.Fori(g0, g1 - (UNROLL - 1), UNROLL) as g:
                        for u in range(UNROLL):
                            step(g + u, u, LATE)
                    continue
                for i in range(PLACES if k > 0 else 0):
                    place_part(k + 1, i)
                    step(g0 + i, i % UNROLL, LATE)
                g0 += PLACES if k > 0 else UNROLL
                with dve.Fori(g0, g0 + MIXED[k + 1] - (UNROLL - 1), UNROLL) as g:
                    for u in range(UNROLL):
                        step(g + u, u, LATE, k + 1, g + (u + BAT0[k + 1] - g0),
                             g * BATCH[k + 1] + (u - g0) * BATCH[k + 1])
                read_sorted(k + 1)
                for g in range(g0 + MIXED[k + 1], g1):
                    step(g, g % UNROLL, LATE)
            for m in range(GROUPS - 4, GROUPS):
                add_segments(m)

            dve.wait_ge(agg_added, GT * GROUPS + 2)
            for b0, b1 in xt_spans:
                a = agg[0][:, b0 * LO:b1 * LO]
                V.tensor_tensor(a, a, agg[1][:, b0 * LO:b1 * LO], ALU.add).then_inc(agg_whole, 1)
            for n, (b0, b1) in enumerate(ln_spans):
                w = b1 - b0
                y3 = y_banks[n % 2][0:LO, 0:w * NF].rearrange("p (b f) -> p b f", b=w)
                dve.wait_ge(y_ready, n + 1)
                then(V.tensor_reduce(stat[:, 3, b0:b1], y3, AX.X, ALU.add))
                then(V.tensor_scalar(stat[:, 0, b0:b1], stat[:, 3, b0:b1], 1.0 / NF, None, ALU.mult))
                V.tensor_tensor(seg(yc, b0, b1), y3, stat[:, 0, b0:b1].unsqueeze(2).to_broadcast([LO, w, NF]),
                                ALU.subtract).then_inc(y_read, 1)
                dve.wait_ge(y_read, n + 1)
                then(V.tensor_tensor(seg(sq, b0, b1), seg(yc, b0, b1), seg(yc, b0, b1), ALU.mult))
                then(V.tensor_reduce(stat[:, 3, b0:b1], seg(sq, b0, b1), AX.X, ALU.add))
            V.tensor_scalar(stat[:, 1, :], stat[:, 3, :], 1.0 / NF, EPS, ALU.mult, ALU.add).then_inc(ln_var, 1)
            dve.wait_ge(ln_sd, 1)
            then(V.reciprocal(stat[:, 0, :], stat[:, 2, :]))
            for b0, b1 in ln_spans:
                V.tensor_tensor(seg(yc, b0, b1), seg(yc, b0, b1),
                                stat[:, 0, b0:b1].unsqueeze(2).to_broadcast([LO, b1 - b0, NF]),
                                ALU.mult).then_inc(ln_done, 1)


_INS = ["x", "src", "dst", "edge_weight1", "L0_gnn_eW1", "L0_gnn_eb1", "L0_gnn_eW2", "L0_gnn_eb2",
        "L0_gnn_nW1", "L0_gnn_nb1", "L0_gnn_nW2", "L0_gnn_nb2"]


def kernel(**inputs):
    import numpy as _np
    import concourse.bacc as _bacc
    from concourse import mybir as _mybir
    from concourse.bass_utils import run_bass_kernel_spmd as _run

    nc = _bacc.Bacc("TRN2", target_bir_lowering=False, num_devices=1)
    arrays, args = {}, []
    for name in _INS:
        a = _np.ascontiguousarray(inputs[name])
        arrays[f"in_{name}_dram"] = a
        args.append(nc.dram_tensor(f"in_{name}_dram", a.shape, _mybir.dt.from_np(a.dtype), kind="ExternalInput").ap())
    args.append(nc.dram_tensor("out_0_dram", (NODES, NF), _mybir.dt.float32, kind="ExternalOutput").ap())
    build(nc, *args)
    r = _run(nc, [arrays], core_ids=[0])
    return r.results[0]["out_0_dram"]
```

```python
from contextlib import ExitStack

import concourse.bass as bass
from concourse import mybir

F32 = mybir.dt.float32
F16 = mybir.dt.float16
BF16 = mybir.dt.bfloat16
I32 = mybir.dt.int32
ALU = mybir.AluOpType
ACT = mybir.ActivationFunctionType
AX = mybir.AxisListType
ENG = mybir.EngineType

NODES, NF, HID = 3125, 64, 128
EDGES = 53125
LO = 125
WIN = NODES // LO
EP = 125
ECOL = EDGES // EP
SLOT = 128
GT = 4
UNROLL = 4
LOAD = [57, 106, 123, 139]
BATCH = [6, 8, 6, 6]
EPS = 1e-5
ROUND = 1.5 * 2.0 ** 23
KEY = 128
SPLITS = 3


def sorted_tiles(cols):
    worst = (EP * cols + WIN * (SLOT - 1)) // SLOT
    step = GT * UNROLL
    return -(-worst // step) * step


TILES = [sorted_tiles(s) for s in LOAD]
CHUNKS = len(LOAD)
COL0 = [sum(LOAD[:k]) for k in range(CHUNKS)]
GRP0 = [sum(TILES[:k]) // GT for k in range(CHUNKS)]
ALL_TILES = sum(TILES)
GROUPS = ALL_TILES // GT
CMAX, SMAX, BMAX = max(TILES), max(LOAD), max(BATCH)
MIXED = [-(-n // b) for n, b in zip(LOAD, BATCH)]
BAT0 = [sum(MIXED[:k]) for k in range(CHUNKS)]
COUNTS, SUMS = 5, 4
assert -(-max(LOAD) // SUMS) <= NF and sum(LOAD) == ECOL and EP * ECOL == EDGES and LO * WIN == NODES
COUNT, OFFSET, ENDS, SUM, SLOTS, WINDOW = "count", "offset", "ends", "sum", "slots", "window"
COUNT_ALL, SUM_ALL = ([(part, i) for i in range(n)] for part, n in ((COUNT, COUNTS), (SUM, SUMS)))
VECTOR_ALL = COUNT_ALL + [(OFFSET, 0)] + SUM_ALL[:3] + [(ENDS, 0)] + SUM_ALL[3:] + [(SLOTS, 0), (WINDOW, 0)]
TENSOR_ALL = [OFFSET, ENDS, WINDOW]
VECTOR_FAST = [COUNT_ALL, [(OFFSET, 0)] + SUM_ALL[:2], [(ENDS, 0), SUM_ALL[2]], [SUM_ALL[3], (SLOTS, 0), (WINDOW, 0)]]
TENSOR_FAST = [[], [OFFSET], [ENDS], [WINDOW]]
VECTOR_SPREAD = [COUNT_ALL[:2], COUNT_ALL[2:3], COUNT_ALL[3:], [], [(OFFSET, 0), SUM_ALL[0]], [SUM_ALL[1]],
                 [(ENDS, 0), SUM_ALL[2]], [SUM_ALL[3]], [(SLOTS, 0), (WINDOW, 0)]]
TENSOR_SPREAD = [[], [], [], [OFFSET], [], [ENDS], [], [WINDOW], []]
VECTOR_PLACES = [None, VECTOR_FAST, VECTOR_SPREAD, VECTOR_SPREAD]
TENSOR_PLACES = [None, TENSOR_FAST, TENSOR_SPREAD, TENSOR_SPREAD]
assert 3 * CMAX <= 512 and WIN % COUNTS == 0 and all(
    len(VECTOR_PLACES[k]) == len(TENSOR_PLACES[k]) <= TILES[k - 1] // GT - MIXED[k] - 2 for k in range(1, CHUNKS))

PLACE_0_AFTER = [0, 3, 6]
SORT_0_AFTER = [9, 10]
PAYLOAD_AFTER = [1, 3]
WC_AFTER = 4
P_AFTER = [6, -(-WIN // 2) - 1]

def batch_size(k, i):
    return min(BATCH[k], LOAD[k] - i * BATCH[k])


def full_batches(k):
    return LOAD[k] // BATCH[k] // UNROLL * UNROLL


XT_W = 4
LN_W = 5

LATE = 99


def spans(n, step):
    return [(a, min(a + step, n)) for a in range(0, n, step)]


def build(nc, x, src, dst, edge_weight, eW1, eb1, eW2, eb2, nW1, nb1, nW2, nb2, out):
    with ExitStack() as ctx:
        def sb(name, shape, dt=F32):
            return ctx.enter_context(nc.sbuf_tensor(name, shape, dt))

        def ps(name, shape, dt=F32):
            return ctx.enter_context(nc.psum_tensor(name, shape, dt))

        def sem(name):
            return ctx.enter_context(nc.semaphore(name))

        q_table = nc.dram_tensor("q_table", [NODES, HID], F32).ap()

        iota_i = sb("iota_i", [128, CMAX], I32)
        part_i = sb("part_i", [128, 1], I32)
        iota_f = sb("iota_f", [128, CMAX])
        iota0_b = sb("iota0_b", [128, CMAX], BF16)
        iota1_b = sb("iota1_b", [128, 128], BF16)
        part_f = sb("part_f", [128, 1])
        ident_f = sb("ident_f", [128, 128])
        ident_b = sb("ident_b", [128, 128], BF16)
        before = sb("before", [128, 128])
        upto = sb("upto", [WIN, WIN])
        ones = sb("ones", [128, 128])
        zeros = sb("zeros", [128, 512])
        ones3 = sb("ones3", [128, 128], BF16)
        w1_sb = sb("w1_sb", [NF + 1, 2 * HID])
        w2_sb = sb("w2_sb", [HID, HID])
        b2_in = sb("b2_in", [SPLITS, HID])
        b2_part = sb("b2_part", [SPLITS, HID], BF16)
        b2_work = sb("b2_work", [SPLITS, 3, HID])
        b2_rows = sb("b2_rows", [128, GT, HID], BF16)
        n1x_sb = sb("n1x_sb", [NF, HID])
        n1a_sb = sb("n1a_sb", [HID, HID])
        nb1_sb = sb("nb1_sb", [HID, 1])
        n2_sb = sb("n2_sb", [HID, NF])
        res_sb = sb("res_sb", [NF + 1, NF])
        wc_in = sb("wc_in", [128, HID])
        wc_part = sb("wc_part", [128, SPLITS, HID], BF16)
        wc_rest = sb("wc_rest", [128, SPLITS, HID])
        x_in_sb = sb("x_in_sb", [128, WIN * NF])
        x_sb = x_in_sb[0:LO, :]
        xT = sb("xT", [NF + 1, NODES])
        pq = sb("pq", [128, WIN * 2 * HID])
        p_table = sb("p_table", [128, WIN, SPLITS, HID], BF16)
        sums = [sb(f"sums{i}", [HID, WIN * HID]) for i in range(2)]
        agg = [t[:, 0:NODES] for t in sums]
        rest = sums[1][0:LO, :]
        src_i = sb("src_i", [EP, ECOL], I32)
        dst_i = sb("dst_i", [EP, ECOL], I32)
        w_in = sb("w_in", [EP, ECOL])
        node_f = sb("node_f", [EP, ECOL])
        lo_f = sb("lo_f", [EP, ECOL])
        win_f = sb("win_f", [EP, ECOL])
        work_e = sb("work_e", [EP, 2, ECOL])
        key_in = sb("key_in", [EP, ECOL, 2, 2], F16)
        weight_in = sb("weight_in", [EP, ECOL, SPLITS, 2], BF16)
        in_win = sb("in_win", [EP, WIN * SMAX], BF16)
        count = sb("count", [EP, WIN * SMAX], BF16)
        scratch = sb("scratch", [EP, 2 * WIN * NF])
        place = scratch[:].rearrange("p (i c) -> p i c", i=2)
        slot = sb("slot", [EP, SMAX])
        slot_t = sb("slot_t", [EP, SMAX])
        col_s = sb("col_s", [EP, SMAX])
        col2 = sb("col2", [EP, SMAX, 2], BF16)
        row2 = sb("row2", [EP, SMAX, 2], BF16)
        total, earlier, all_edges, win_tiles, tiles_upto, tiles_before, base, run_end, round_tmp = (
            sb(name, [EP, WIN]) for name in (
                "total", "earlier", "all_edges", "win_tiles", "tiles_upto", "tiles_before", "base", "run_end",
                "round_tmp"))
        win_tiles_c, tiles_upto_c, round_tmp_c = (
            sb(name, [WIN, 1]) for name in ("win_tiles_c", "tiles_upto_c", "round_tmp_c"))
        ge = sb("ge", [WIN, CMAX])
        row_hot = sb("row_hot", [EP, 2, BMAX, SLOT], BF16)
        col_hot = sb("col_hot", [EP, 2, BMAX, CMAX], BF16)
        key_hot = sb("key_hot", [EP, 2, BMAX, 2, CMAX], F16)
        weight_hot = sb("weight_hot", [EP, 2, BMAX, SPLITS, CMAX], BF16)
        odd = x_in_sb[:, 0:CMAX]
        key_s = x_in_sb[:, CMAX:3 * CMAX].rearrange("p (v c) -> p v c", v=2)
        turn = sb("turn", [1, ALL_TILES])
        lo2 = sb("lo2", [128, ALL_TILES, 2], BF16)
        w_parts = sb("w_parts", [128, ALL_TILES, SPLITS], BF16)
        q_index = sb("q_index", [128, ALL_TILES])
        rows_at = sb("rows_at", [128, 4, GT], I32)
        p_at = sb("p_at", [1, ALL_TILES], I32)
        agg_at = sb("agg_at", [1, ALL_TILES], I32)
        h1 = pq[:, 2048:3072].rearrange("p (g e) -> p g e", g=2)
        e2 = pq[:, 3072:4096].rearrange("p (g e) -> p g e", g=2)
        q_rows = pq[:, 4096:6144].rearrange("p (g j f) -> p g j f", g=4, j=GT)
        hot = sb("hot", [128, 2, GT, 128], BF16)
        hot32 = pq[:, 0:4 * GT * LO].rearrange("p (g j f) -> p g j f", g=4, j=GT)
        hotT = sb("hotT", [128, 2, GT * 128], BF16)
        hT = pq
        yc = scratch[:, 0:WIN * NF].rearrange("p (b f) -> p b f", b=WIN)
        sq = scratch[:, WIN * NF:2 * WIN * NF].rearrange("p (b f) -> p b f", b=WIN)
        stat = sb("stat", [LO, 4, WIN])
        eps_sb = sb("eps_sb", [LO, 1])

        sort_ps = ps("sort_ps", [128, 512])
        weight_ps = ps("weight_ps", [128, 512])
        hotT_ps = ps("hotT_ps", [128, GT * 128], BF16)
        pre_ps = [ps(f"pre_ps{i}", [128, 512]) for i in range(2)]
        e_ps = [ps(f"e_ps{i}", [128, 512]) for i in range(2)]
        seg_ps = ps("seg_ps", [128, 512])
        y_banks = [sort_ps, seg_ps]
        hid_banks = [sort_ps, weight_ps] + pre_ps + e_ps + [weight_ps]
        work_ps = [pre_ps[0], pre_ps[1], e_ps[0], e_ps[1]]

        src_in, dst_in, w_in_sem, x_in, w_loaded, wc_loaded = (
            sem(n) for n in ("src_in", "dst_in", "w_in_sem", "x_in", "w_loaded", "wc_loaded"))
        iotas_ready = sem("iotas_ready")
        fills_ready = sem("fills_ready")
        v_done = sem("v_done")
        ident_ready = sem("ident_ready")
        xT_ps_ready = sem("xT_ps_ready")
        xT_copied = sem("xT_copied")
        pq_ps_ready = sem("pq_ps_ready")
        pq_copied = sem("pq_copied")
        wc_step = sem("wc_step")
        wc_first = sem("wc_first")
        wc_placed = sem("wc_placed")
        payload_ready = sem("payload_ready")
        payload_in = sem("payload_in")
        p_part = sem("p_part")
        p_rest = sem("p_rest")
        q_stored = sem("q_stored")
        b2_step = sem("b2_step")
        b2_ready = sem("b2_ready")
        totals_ready = sem("totals_ready")
        offsets_ready = sem("offsets_ready")
        round_ready = sem("round_ready")
        pads_ready = sem("pads_ready")
        ends_ready = sem("ends_ready")
        ge_ready = sem("ge_ready")
        window_ready = sem("window_ready")
        slots_ready = sem("slots_ready")
        cols_ready = sem("cols_ready")
        hots_ready = sem("hots_ready")
        sort_mm = sem("sort_mm")
        sorted_ready = sem("sorted_ready")
        tables_ready = sem("tables_ready")
        rows_in = [sem(f"rows_in{i}") for i in range(4)]
        staged = sem("staged")
        hot_ready = sem("hot_ready")
        hotT_ps_ready = sem("hotT_ps_ready")
        hot32_ready = sem("hot32_ready")
        hotT_ready = sem("hotT_ready")
        pre_ready = sem("pre_ready")
        h1_ready = sem("h1_ready")
        e_ready = sem("e_ready")
        e2_ready = sem("e2_ready")
        seg_ready = sem("seg_ready")
        agg_clear = sem("agg_clear")
        agg_added = sem("agg_added")
        agg_whole = sem("agg_whole")
        hid_ps_ready = sem("hid_ps_ready")
        hid_ready = sem("hid_ready")
        y_ready = sem("y_ready")
        y_read = sem("y_read")
        eps_ready = sem("eps_ready")
        ln_var = sem("ln_var")
        ln_sd = sem("ln_sd")
        ln_done = sem("ln_done")
        out_stored = sem("out_stored")

        HOTS = 1 + 2 + SPLITS

        xt_spans, ln_spans = spans(WIN, XT_W), spans(WIN, LN_W)
        pq_spans = spans(WIN, 2)
        p_spans = [(0, pq_spans[P_AFTER[0]][1]), (pq_spans[P_AFTER[0]][1], WIN)]
        rest3 = rest.rearrange("p (b h) -> p b h", b=WIN)

        FILLS = 7
        W_LOADS = 10

        block = ctx.enter_context(nc.Block())

        @block.sync
        def _(sp):
            sp.dma_start(src_i[:], src.rearrange("(p t) -> p t", p=EP)).then_inc(src_in, 16)
            sp.dma_start(dst_i[:], dst.rearrange("(p t) -> p t", p=EP)).then_inc(dst_in, 16)
            sp.dma_start(w_in[:], edge_weight.rearrange("(p t) o -> p (t o)", p=EP)).then_inc(w_in_sem, 16)
            sp.wait_ge(pq_copied, len(pq_spans))
            sp.dma_start(q_table.rearrange("(p b) f -> p b f", b=WIN),
                         pq[0:LO, :].rearrange("p (b h) -> p b h", b=WIN)[:, :, HID:2 * HID]).then_inc(q_stored, 16)
            for n, (b0, b1) in enumerate(ln_spans):
                sp.wait_ge(ln_done, n + 1)
                sp.dma_start(out.rearrange("(p b) f -> p b f", b=WIN)[:, b0:b1, :],
                             yc[:, b0:b1, :]).then_inc(out_stored, 16)
            sp.wait_ge(out_stored, 16 * len(ln_spans))

        @block.scalar
        def _(act):
            act.dma_start(x_sb, x.rearrange("(p b) f -> p (b f)", b=WIN)).then_inc(x_in, 16)
            act.dma_start(w1_sb[0:NF, 0:HID], eW1[0:NF, :]).then_inc(w_loaded, 16)
            act.dma_start(w1_sb[0:NF, HID:2 * HID], eW1[NF:2 * NF, :]).then_inc(w_loaded, 16)
            act.dma_start(w1_sb[NF:NF + 1, 0:HID], eb1.rearrange("(a f) -> a f", a=1)).then_inc(w_loaded, 16)
            act.dma_start(wc_in[96:128, :], eW1[2 * NF:2 * NF + 1, :].to_broadcast([32, HID])).then_inc(wc_loaded, 16)
            act.dma_start(b2_in[:], eb2.rearrange("(a f) -> a f", a=1).to_broadcast([SPLITS, HID])).then_inc(w_loaded, 16)
            act.dma_start(w2_sb[:], eW2).then_inc(w_loaded, 16)
            act.dma_start(n1x_sb[:], nW1[0:NF, :]).then_inc(w_loaded, 16)
            act.dma_start(n1a_sb[:], nW1[NF:NF + HID, :]).then_inc(w_loaded, 16)
            act.dma_start(nb1_sb[:], nb1.rearrange("(f a) -> f a", a=1)).then_inc(w_loaded, 16)
            act.dma_start(n2_sb[:], nW2).then_inc(w_loaded, 16)
            act.dma_start(res_sb[NF:NF + 1, :], nb2.rearrange("(a f) -> a f", a=1)).then_inc(w_loaded, 16)

            def write_twice(t, v, values):
                nc.scalar.activation(t[:, :, v, :], values.unsqueeze(2).to_broadcast([EP, ECOL, 2]),
                                     ACT.Copy).then_inc(payload_in, 1)

            def place_wc(s):
                act.wait_ge(wc_step, 2 * s + 1)
                nc.scalar.activation(p_table[96:128, :, s, :],
                                     wc_part[96:128, s, :].unsqueeze(1).to_broadcast([32, WIN, HID]),
                                     ACT.Copy).then_inc(wc_placed, 1)
                act.wait_ge(wc_placed, s)

            def split_p(half, s):
                a, b = p_spans[half]
                left = pq[0:LO, :].rearrange("p (b h) -> p b h", b=WIN)[:, a:b, 0:HID] if s == 0 else rest3[:, a:b, :]
                nc.scalar.activation(p_table[0:LO, a:b, s, :], left, ACT.Copy).then_inc(p_part, 1)

            act.wait_ge(w_in_sem, 16)
            write_twice(weight_in, 0, w_in[:])
            for n, (b0, b1) in enumerate(xt_spans):
                act.wait_ge(xT_ps_ready, n + 1)
                nc.scalar.activation(xT[0:NF, b0 * LO:b1 * LO], work_ps[n % 4][0:NF, 0:(b1 - b0) * LO],
                                     ACT.Copy).then_inc(xT_copied, 1)
            act.wait_ge(payload_ready, 1)
            write_twice(weight_in, 1, w_in[:])
            for n, (b0, b1) in enumerate(pq_spans):
                act.wait_ge(pq_ps_ready, n + 1)
                nc.scalar.activation(pq[0:LO, b0 * 2 * HID:b1 * 2 * HID],
                                     work_ps[(n + 3) % 4][0:LO, 0:(b1 - b0) * 2 * HID], ACT.Copy).then_inc(pq_copied, 1)
                if n == PAYLOAD_AFTER[0]:
                    act.wait_ge(payload_ready, 2)
                    write_twice(key_in, 0, work_e[:, 0, :])
                    write_twice(key_in, 1, work_e[:, 1, :])
                if n == PAYLOAD_AFTER[1]:
                    act.wait_ge(payload_ready, 3)
                    write_twice(weight_in, 2, w_in[:])
                if n == WC_AFTER:
                    place_wc(1)
                if n in P_AFTER:
                    half = P_AFTER.index(n)
                    act.wait_ge(wc_first, 1)
                    act.wait_ge(pq_copied, n + 1)
                    split_p(half, 0)
            place_wc(2)
            for s in range(1, SPLITS):
                for half in range(len(P_AFTER)):
                    act.wait_ge(p_rest, len(P_AFTER) * (s - 1) + half + 1)
                    split_p(half, s)

            def convert(g, u, n):
                act.wait_ge(hot_ready, 2 * g + 2)
                if n >= 4:
                    act.wait_ge(seg_ready, g - 3)
                nc.scalar.activation(hot32[:, u % 4], hot[:, u % 2, :, 0:LO], ACT.Copy).then_inc(hot32_ready, 1)

            def turned(g, u, n):
                act.wait_ge(hotT_ps_ready, g + 1)
                if n >= 2:
                    act.wait_ge(pre_ready, g - 1)
                nc.scalar.activation(hotT[:, u % 2, :], hotT_ps[:], ACT.Copy).then_inc(hotT_ready, 1)

            def silu1(m, u, n):
                act.wait_ge(pre_ready, m + 1)
                if n >= 3:
                    act.wait_ge(e_ready, m - 1)
                nc.scalar.activation(h1[:, u % 2, :], pre_ps[u % 2][:], ACT.Silu).then_inc(h1_ready, 1)

            def silu2(m, u, n):
                act.wait_ge(e_ready, m + 1)
                if n >= 4:
                    act.wait_ge(seg_ready, m - 1)
                nc.scalar.activation(e2[:, u % 2, :], e_ps[u % 2][:], ACT.Silu).then_inc(e2_ready, 1)

            def stage(g, u, n):
                if n >= 4:
                    act.wait_ge(pre_ready, g - 3)
                at = q_index[:, GT * g:GT * g + GT] if isinstance(g, int) else q_index[:, bass.ds(g * GT, GT)]
                nc.scalar.activation(rows_at[:, u % 4, :], at, ACT.Copy).then_inc(staged, 1)

            def step(g, u, n, staging=True, tables=None):
                convert(g, u, n)
                turned(g, u, n)
                if n >= 1:
                    silu1(g - 1, u + 3, n)
                if n >= 2:
                    silu2(g - 2, u + 2, n)
                if tables is not None:
                    act.wait_ge(tables_ready, tables)
                if staging:
                    stage(g + 3, u + 3, n + 3)

            act.wait_ge(q_stored, 16)
            act.wait_ge(tables_ready, 1)
            for g in range(3):
                stage(g, g, g)
            for g in range(UNROLL):
                step(g, g, g)
            for k in range(CHUNKS):
                a, b = GRP0[k] + UNROLL * (k == 0), GRP0[k] + TILES[k] // GT - UNROLL
                with act.Fori(a, b - (UNROLL - 1), UNROLL) as g:
                    for u in range(UNROLL):
                        step(g + u, u, LATE)
                if k + 1 < CHUNKS:
                    for u in range(UNROLL):
                        step(b + u, u, LATE, tables=k + 2 if u == 1 else None)
            for u in range(UNROLL):
                step(GROUPS - UNROLL + u, u, LATE, u == 0)
            silu1(GROUPS - 1, UNROLL + 3, LATE)
            silu2(GROUPS - 2, UNROLL + 2, LATE)
            silu2(GROUPS - 1, UNROLL + 3, LATE)

            for n, (b0, b1) in enumerate(xt_spans):
                act.wait_ge(hid_ps_ready, n + 1)
                nc.scalar.activation(hT[:, b0 * LO:b1 * LO], hid_banks[n][:, 0:(b1 - b0) * LO], ACT.Silu,
                                     bias=nb1_sb[:, 0:1]).then_inc(hid_ready, 1)
            for n, (b0, b1) in enumerate(ln_spans):
                act.wait_ge(y_read, n + 1)
                for b in range(b0, b1):
                    nc.scalar.activation(sq[:, b, :], yc[:, b, :], ACT.Square,
                                         accum_out=stat[:, 1, b:b + 1]).then_inc(ln_var, 1)
            act.wait_ge(ln_var, WIN)
            act.wait_ge(eps_ready, 1)
            nc.scalar.activation(stat[:, 2, :], stat[:, 1, :], ACT.Sqrt, bias=eps_sb[:, 0:1],
                                 scale=1.0 / NF).then_inc(ln_sd, 1)

        @block.gpsimd
        def _(pool):
            nc.gpsimd.iota(part_i[:], pattern=[[0, 1]], base=0, channel_multiplier=1).then_inc(iotas_ready, 1)
            nc.gpsimd.iota(iota_i[:], pattern=[[1, CMAX]], base=0, channel_multiplier=0).then_inc(iotas_ready, 1)
            fills = [(ones[:], 1.0), (ones3[:], 0.0), (zeros[:], 0.0),
                     (b2_rows[:], 0.0), (w1_sb[NF:NF + 1, HID:2 * HID], 0.0), (xT[NF:NF + 1, :], 1.0),
                     (ones3[0:SPLITS, :], 1.0)]
            for n, (t, value) in enumerate(fills):
                pool.wait_ge(fills_ready, n)
                nc.gpsimd.memset(t, value).then_inc(fills_ready, 1)
            pool.wait_ge(fills_ready, FILLS)
            nc.gpsimd.memset(agg[0], 0.0).then_inc(agg_clear, 1)

            pool.wait_ge(wc_loaded, 16)
            pool.wait_ge(agg_clear, 1)
            for s in range(SPLITS):
                left = wc_in[96:128, :] if s == 0 else wc_rest[96:128, s - 1, :]
                nc.gpsimd.tensor_copy(wc_part[96:128, s, :], left).then_inc(wc_step, 1)
                pool.wait_ge(wc_step, 2 * s + 1)
                nc.gpsimd.tensor_tensor(wc_rest[96:128, s, :], left, wc_part[96:128, s, :], ALU.subtract).then_inc(wc_step, 1)
                pool.wait_ge(wc_step, 2 * s + 2)
            nc.gpsimd.tensor_copy(p_table[96:128, :, 0, :],
                                  wc_part[96:128, 0, :].unsqueeze(1).to_broadcast([32, WIN, HID])).then_inc(wc_first, 1)

            small_steps = [0]

            def then(ins):
                small_steps[0] += 1
                ins.then_inc(b2_step, 1)
                pool.wait_ge(b2_step, small_steps[0])

            pool.wait_ge(w_loaded, 16 * W_LOADS)
            pool.wait_ge(ident_ready, 1)
            then(nc.gpsimd.tensor_copy(res_sb[0:NF, :], ident_f[0:NF, 0:NF]))
            for s in range(SPLITS):
                left = b2_in[:] if s == 0 else b2_work[:, 1, :]
                then(nc.gpsimd.tensor_copy(b2_part[:], left))
                then(nc.gpsimd.tensor_tensor(b2_work[:, 1, :], left, b2_part[:], ALU.subtract))
                one_row = ident_f[0:SPLITS, s:s + 1].to_broadcast([SPLITS, HID])
                if s == 0:
                    then(nc.gpsimd.tensor_tensor(b2_work[:, 0, :], b2_part[:], one_row, ALU.mult))
                else:
                    then(nc.gpsimd.tensor_tensor(b2_work[:, 2, :], b2_part[:], one_row, ALU.mult))
                    then(nc.gpsimd.tensor_tensor(b2_work[:, 0, :], b2_work[:, 0, :], b2_work[:, 2, :], ALU.add))
            nc.gpsimd.tensor_copy(b2_rows[0:SPLITS], b2_work[:, 0, :].unsqueeze(1).to_broadcast([SPLITS, GT, HID])) \
                .then_inc(b2_ready, 1)

            for s in range(SPLITS - 1):
                for half, (a, b) in enumerate(p_spans):
                    pool.wait_ge(p_part, len(p_spans) * s + half + 1)
                    left = pq[0:LO, :].rearrange("p (b h) -> p b h", b=WIN)[:, a:b, 0:HID] if s == 0 else rest3[:, a:b, :]
                    nc.gpsimd.tensor_tensor(rest3[:, a:b, :], left, p_table[0:LO, a:b, s, :],
                                            ALU.subtract).then_inc(p_rest, 1)

            nc.gpsimd.memset(eps_sb[:], EPS).then_inc(eps_ready, 1)
            pool.wait_ge(p_part, SPLITS * len(p_spans))
            nc.gpsimd.memset(agg[1], 0.0).then_inc(agg_added, 2)

            def gather(g, u):
                pool.wait_ge(staged, g + 2)
                nc.gpsimd.tensor_copy(turn[:, bass.ds(g * GT, 1)], q_index[0:1, bass.ds(g * GT, 1)])
                for v in (u, u + 1):
                    for j in range(GT):
                        nc.gpsimd.indirect_dma_start(
                            q_rows[:, v, j, :], None, q_table,
                            bass.IndirectOffsetOnAxis(ap=rows_at[:, v, j:j + 1], axis=0)).then_inc(rows_in[v], 16)

            pool.wait_ge(q_stored, 16)
            with pool.Fori(0, GROUPS - (UNROLL - 1), UNROLL) as g:
                for u in range(0, UNROLL, 2):
                    gather(g + u, u)

        @block.tensor
        def _(pe):
            def mm(o, lhsT, rhs, start, stop, **kw):
                return nc.tensor.matmul(o, lhsT, rhs, start=start, stop=stop, **kw)

            def place_part(k, part):
                if part == OFFSET:
                    pe.wait_ge(totals_ready, k + 1)
                    tot = total[:]
                    mm(sort_ps[0:EP, 0:WIN], before[0:EP, 0:EP], tot, True, True)
                    mm(sort_ps[0:EP, 32:32 + WIN], ones[0:EP, 0:EP], tot, True, True)
                    mm(sort_ps[0:WIN, 64:65], tot, ones[0:EP, 0:1], True, True).then_inc(offsets_ready, 1)
                elif part == ENDS:
                    pe.wait_ge(pads_ready, k + 1)
                    mm(sort_ps[0:WIN, 96:97], upto[:], win_tiles_c[:], True, True).then_inc(ends_ready, 1)
                elif part == WINDOW:
                    pe.wait_ge(ge_ready, k + 1)
                    mm(sort_ps[0:1, 128:128 + TILES[k]], ones[0:WIN - 1, 0:1], ge[0:WIN - 1, 0:TILES[k]],
                       True, True).then_inc(window_ready, 1)

            def sort_sums(k, q, b, start, stop):
                c = TILES[k]
                rows = row_hot[:, q, b, :] if b is not None else zeros[0:EP, 0:128]
                keys = key_hot[:, q, b, :, 0:c] if b is not None else zeros[0:EP, 0:2 * c]
                weights = weight_hot[:, q, b, :, 0:c] if b is not None else zeros[0:EP, 0:3 * c]
                mm(sort_ps[:, 0:2 * c], rows, keys, start, stop)
                return mm(weight_ps[:, 0:3 * c], rows, weights, start, stop)

            def sort_open(k):
                pe.wait_ge(slots_ready, k + 1)
                sort_sums(k, 0, None, True, False)

            def sort_batch(k, n, q, size):
                pe.wait_ge(hots_ready, HOTS * n + HOTS)
                for b in range(size):
                    last = sort_sums(k, q, b, False, False)
                last.then_inc(sort_mm, 1)

            def sort_close(k):
                sort_sums(k, 0, None, False, True).then_inc(sorted_ready, 1)

            pe.wait_ge(x_in, 16)
            pe.wait_ge(ident_ready, 1)
            for n, (b0, b1) in enumerate(xt_spans):
                if n >= 4:
                    pe.wait_ge(xT_copied, n - 3)
                for b in range(b0, b1):
                    last = nc.tensor.transpose(work_ps[n % 4][0:NF, (b - b0) * LO:(b - b0 + 1) * LO],
                                               x_sb[:, b * NF:(b + 1) * NF], ident_f[0:LO, 0:LO])
                last.then_inc(xT_ps_ready, 1)
            pe.wait_ge(w_loaded, 16 * W_LOADS)
            pe.wait_ge(fills_ready, FILLS)
            for n, (b0, b1) in enumerate(pq_spans):
                pe.wait_ge(xT_copied, max(-(-b1 // XT_W), min(n + 4, len(xt_spans))))
                if n >= 4:
                    pe.wait_ge(pq_copied, n - 3)
                for b in range(b0, b1):
                    last = mm(work_ps[(n + 3) % 4][0:LO, (b - b0) * 2 * HID:(b - b0 + 1) * 2 * HID],
                              xT[:, b * LO:(b + 1) * LO], w1_sb[:], True, True)
                last.then_inc(pq_ps_ready, 1)
                if n in PLACE_0_AFTER:
                    place_part(0, TENSOR_ALL[PLACE_0_AFTER.index(n)])
                if n in SORT_0_AFTER:
                    i = SORT_0_AFTER.index(n)
                    if i == 0:
                        sort_open(0)
                    sort_batch(0, i, i % 2, BATCH[0])

            loop = full_batches(0)
            for n in range(len(SORT_0_AFTER), UNROLL):
                sort_batch(0, n, n % 2, BATCH[0])
            with pe.Fori(UNROLL, loop - (UNROLL - 1), UNROLL) as n:
                for q in range(UNROLL):
                    sort_batch(0, n + q, q % 2, BATCH[0])
            for n in range(loop, MIXED[0]):
                sort_batch(0, n, n % 2, batch_size(0, n))
            sort_close(0)

            def turn(g, u, n):
                pe.wait_ge(hot_ready, 2 * g + 2)
                if n >= 1:
                    pe.wait_ge(hotT_ready, g)
                for j in range(GT):
                    last = nc.tensor.transpose(hotT_ps[:, j * 128:(j + 1) * 128], hot[:, u % 2, j, :], ident_b[:])
                last.then_inc(hotT_ps_ready, 1)

            def tile_windows(m):
                at = p_at[0:1, GT * m:GT * m + GT] if isinstance(m, int) else p_at[0:1, bass.ds(m * GT, GT)]
                return nc.values_load_multi_w_load_instructions(
                    at, engines=(ENG.PE,), min_val=0, max_val=(WIN - 1) * SPLITS * HID,
                    skip_runtime_bounds_check_because="a window's number is a count of 24 comparisons")[1]

            p_flat = p_table[:].rearrange("p b s f -> p (b s f)")

            def first_layer(m, u, n):
                windows = tile_windows(m)
                pe.wait_ge(rows_in[u % 4], rows_count(m, u))
                pe.wait_ge(hotT_ready, m + 1)
                if n >= 3:
                    pe.wait_ge(h1_ready, m - 1)
                for j in range(GT):
                    o = pre_ps[u % 2][:, j * 128:(j + 1) * 128]
                    mm(o, q_rows[:, u % 4, j, :], ident_f[:], True, False, is_transpose=True)
                    for s in range(SPLITS):
                        last = mm(o, p_flat[:, bass.ds(windows[j] + s * HID, HID)],
                                  hotT[:, u % 2, j * 128:(j + 1) * 128], False, s == SPLITS - 1)
                last.then_inc(pre_ready, 1)

            def rows_count(m, u):
                if isinstance(m, int):
                    return 16 * GT * (m // 4 + 1)
                return (m - u % 4) * (16 * GT // 4) + 16 * GT

            def second_layer(m, u, n):
                pe.wait_ge(h1_ready, m + 1)
                if n >= 4:
                    pe.wait_ge(e2_ready, m - 1)
                mm(e_ps[u % 2][:], ones3[:], b2_rows[:].rearrange("p j f -> p (j f)"), True, False)
                for j in range(GT):
                    last = mm(e_ps[u % 2][:, j * HID:(j + 1) * HID], h1[:, u % 2, j * 128:(j + 1) * 128], w2_sb[:],
                              False, j == GT - 1)
                last.then_inc(e_ready, 1)

            def segment(m, u, n):
                pe.wait_ge(e2_ready, m + 1)
                pe.wait_ge(hot32_ready, m + 1)
                if n >= 4:
                    pe.wait_ge(agg_added, m * GT + 2)
                for j in range(GT):
                    last = mm(seg_ps[:, j * LO:(j + 1) * LO], e2[:, u % 2, j * HID:(j + 1) * HID],
                              hot32[:, u % 4, j, :], True, True)
                last.then_inc(seg_ready, 1)

            def step(g, u, n, k=None, batch=None, q=None, size=None):
                turn(g, u, n)
                if n >= 1:
                    first_layer(g - 1, u + 3, n)
                if k is not None:
                    sort_batch(k, batch, q, size)
                if n >= 2:
                    second_layer(g - 2, u + 2, n)
                if n >= 3:
                    segment(g - 3, u + 1, n)

            pe.wait_ge(p_part, SPLITS * len(p_spans))
            pe.wait_ge(b2_ready, 1)
            pe.wait_ge(tables_ready, 1)
            for k in range(CHUNKS):
                g0, g1 = GRP0[k], GRP0[k] + TILES[k] // GT
                pe.wait_ge(tables_ready, k + 1)
                if k + 1 == CHUNKS:
                    with pe.Fori(g0, g1 - (UNROLL - 1), UNROLL) as g:
                        for u in range(UNROLL):
                            step(g + u, u, LATE)
                    continue
                for i, parts in enumerate(TENSOR_PLACES[k + 1]):
                    for part in parts:
                        place_part(k + 1, part)
                    step(g0 + i, i % UNROLL, g0 + i)
                g0 += len(TENSOR_PLACES[k + 1])
                loop, shift = full_batches(k + 1), BAT0[k + 1] - g0
                sort_open(k + 1)
                with pe.Fori(g0, g0 + loop - (UNROLL - 1), UNROLL) as g:
                    for u in range(UNROLL):
                        step(g + u, (g0 + u) % UNROLL, LATE, k + 1, g + (u + shift), (BAT0[k + 1] + u) % 2, BATCH[k + 1])
                for i in range(loop, MIXED[k + 1]):
                    n = BAT0[k + 1] + i
                    step(g0 + i, (g0 + i) % UNROLL, LATE, k + 1, n, n % 2, batch_size(k + 1, i))
                sort_close(k + 1)
                for g in range(g0 + MIXED[k + 1], g1):
                    step(g, g % UNROLL, LATE)

            def hidden_x(n):
                b0, b1 = xt_spans[n]
                mm(hid_banks[n][:, 0:(b1 - b0) * LO], n1x_sb[:], xT[0:NF, b0 * LO:b1 * LO], True, False)

            u = UNROLL
            first_layer(GROUPS - 1, u + 3, LATE)
            second_layer(GROUPS - 2, u + 2, LATE)
            hidden_x(0)
            segment(GROUPS - 3, u + 1, LATE)
            hidden_x(1)
            second_layer(GROUPS - 1, u + 3, LATE)
            hidden_x(2)
            segment(GROUPS - 2, u + 2, LATE)
            hidden_x(3)
            hidden_x(4)
            segment(GROUPS - 1, u + 3, LATE)
            hidden_x(5)

            for n, (b0, b1) in enumerate(xt_spans):
                o = hid_banks[n][:, 0:(b1 - b0) * LO]
                if n >= 6:
                    pe.wait_ge(hid_ready, n - 4)
                    hidden_x(n)
                pe.wait_ge(agg_whole, n + 1)
                mm(o, n1a_sb[:], agg[0][:, b0 * LO:b1 * LO], False, True).then_inc(hid_ps_ready, 1)
            for n, (b0, b1) in enumerate(ln_spans):
                pe.wait_ge(hid_ready, -(-b1 // XT_W))
                if n >= len(y_banks):
                    pe.wait_ge(y_read, n - len(y_banks) + 1)
                for b in range(b0, b1):
                    o = y_banks[n % len(y_banks)][0:LO, (b - b0) * NF:(b - b0 + 1) * NF]
                    mm(o, hT[:, b * LO:(b + 1) * LO], n2_sb[:], True, False)
                    last = mm(o, xT[:, b * LO:(b + 1) * LO], res_sb[:], False, True)
                last.then_inc(y_ready, 1)

        @block.vector
        def _(dve):
            V = nc.vector
            steps = [0]

            def then(ins):
                steps[0] += 1
                ins.then_inc(v_done, 1)
                dve.wait_ge(v_done, steps[0])

            def mark(ins):
                steps[0] += 1
                ins.then_inc(v_done, 1)
                return steps[0]

            def done(step):
                dve.wait_ge(v_done, step)

            def scaled_round(dst, tmp, src, scale, shift):
                then(V.tensor_scalar(tmp, src, scale, shift, ALU.mult, ALU.add))
                then(V.tensor_scalar(dst, tmp, ROUND, -ROUND, ALU.add, ALU.add))

            dve.wait_ge(iotas_ready, 2)
            then(V.tensor_copy(iota_f[:], iota_i[:]))
            then(V.tensor_copy(part_f[:], part_i[:]))
            V.tensor_scalar(ident_f[:], iota_f[:, 0:128], part_f[:, 0:1], None, ALU.is_equal).then_inc(ident_ready, 1)
            dve.wait_ge(ident_ready, 1)
            then(V.tensor_copy(ident_b[:], ident_f[:]))
            then(V.tensor_scalar(before[:], iota_f[:, 0:128], part_f[:, 0:1], None, ALU.is_gt))
            then(V.tensor_scalar(upto[:], iota_f[0:WIN, 0:WIN], part_f[0:WIN, 0:1], None, ALU.is_ge))
            then(V.tensor_scalar(iota1_b[:], iota_f[:, 0:128], 1.0, None, ALU.add))
            then(V.tensor_copy(iota0_b[:], iota_f[:]))

            dve.wait_ge(src_in, 16)
            then(V.tensor_copy(node_f[:], src_i[:]))
            scaled_round(lo_f[:], win_f[:], node_f[:], 1.0 / WIN, -(WIN // 2) / WIN)
            then(V.scalar_tensor_tensor(win_f[:], lo_f[:], -float(WIN), node_f[:], ALU.mult, ALU.add))

            def twice(ap):
                return ap.unsqueeze(2).to_broadcast([EP, ap.shape[1], 2])

            def payload():
                half, rem, left = work_e[:, 0, :], work_e[:, 1, :], w_in[:]
                dve.wait_ge(dst_in, 16)
                then(V.tensor_copy(node_f[:], dst_i[:]))
                dve.wait_ge(payload_in, 1)
                V.tensor_tensor(left, left, weight_in[:, :, 0, 0], ALU.subtract).then_inc(payload_ready, 1)
                scaled_round(half, rem, node_f[:], 0.5, -0.25)
                then(V.scalar_tensor_tensor(rem, half, -2.0, node_f[:], ALU.mult, ALU.add))
                then(V.tensor_scalar(rem, rem, float(KEY), 1.0, ALU.mult, ALU.add))
                V.tensor_tensor(rem, rem, lo_f[:], ALU.add).then_inc(payload_ready, 1)

            def payload_end():
                left = w_in[:]
                dve.wait_ge(payload_ready, 1)
                dve.wait_ge(payload_in, 2)
                V.tensor_tensor(left, left, weight_in[:, :, 1, 0], ALU.subtract).then_inc(payload_ready, 1)

            matched, added, summed = {}, {}, {}

            def place_part(k, part, i):
                n, c0, c, t0 = LOAD[k], COL0[k], TILES[k], GT * GRP0[k]
                win3, count3 = (t[:, 0:WIN * n].rearrange("p (b t) -> p b t", b=WIN) for t in (in_win, count))
                if part == COUNT:
                    def match(i):
                        b0, b1 = WIN // COUNTS * i, WIN // COUNTS * (i + 1)
                        shape = [EP, b1 - b0, n]
                        matched[i] = mark(V.tensor_tensor(
                            win3[:, b0:b1, :], win_f[:, c0:c0 + n].unsqueeze(1).to_broadcast(shape),
                            iota_f[0:EP, b0:b1].unsqueeze(2).to_broadcast(shape), ALU.is_equal))

                    if i == 0:
                        match(0)
                    if i + 1 < COUNTS:
                        match(i + 1)
                    a, b = WIN // COUNTS * i * n, WIN // COUNTS * (i + 1) * n
                    done(matched[i])
                    last = mark(V.tensor_tensor_scan(count[:, a:b], ones[0:EP, 0:1].to_broadcast([EP, b - a]),
                                                     in_win[:, a:b], 0.0, ALU.mult, ALU.add))
                    if i == COUNTS - 1:
                        done(last)
                        then(V.tensor_copy(run_end[:], count3[:, :, n - 1]))
                        then(V.tensor_copy(total[:], run_end[:]))
                        runs, totals = (t[:].rearrange("p (i b) -> p i b", i=COUNTS) for t in (run_end, total))
                        V.tensor_tensor(totals[:, :, 1:], runs[:, :, 1:], runs[:, :, 0:WIN // COUNTS - 1],
                                        ALU.subtract).then_inc(totals_ready, 1)
                elif part == OFFSET:
                    dve.wait_ge(offsets_ready, k + 1)
                    then(V.tensor_copy(earlier[:], sort_ps[0:EP, 0:WIN]))
                    then(V.tensor_copy(all_edges[:], sort_ps[0:EP, 32:32 + WIN]))
                    V.tensor_scalar(round_tmp_c[:], sort_ps[0:WIN, 64:65], 1.0 / SLOT, (SLOT / 2 - 0.5) / SLOT,
                                    ALU.mult, ALU.add).then_inc(round_ready, 1)
                    dve.wait_ge(round_ready, k + 1)
                    V.tensor_scalar(win_tiles_c[:], round_tmp_c[:], ROUND, -ROUND,
                                    ALU.add, ALU.add).then_inc(pads_ready, 1)
                    scaled_round(win_tiles[:], round_tmp[:], all_edges[:],
                                 1.0 / SLOT, (SLOT / 2 - 0.5) / SLOT)
                    then(V.tensor_tensor_scan(tiles_upto[:], ones[0:EP, 0:WIN], win_tiles[:], 0.0,
                                              ALU.mult, ALU.add))
                    then(V.tensor_tensor(tiles_before[:], tiles_upto[:], win_tiles[:], ALU.subtract))
                    then(V.scalar_tensor_tensor(base[:], tiles_before[:], float(SLOT),
                                                earlier[:], ALU.mult, ALU.add))
                    then(V.tensor_tensor(base[:], base[:], run_end[:], ALU.subtract))
                    then(V.tensor_tensor(base[:], base[:], total[:], ALU.add))
                elif part == ENDS:
                    dve.wait_ge(ends_ready, k + 1)
                    then(V.tensor_copy(tiles_upto_c[:], sort_ps[0:WIN, 96:97]))
                    V.tensor_scalar(ge[0:WIN - 1, 0:c], iota_f[0:WIN - 1, 0:c], tiles_upto_c[0:WIN - 1, :], None,
                                    ALU.is_ge).then_inc(ge_ready, 1)
                elif part == SUM:
                    size = -(-n // SUMS)

                    def places(i):
                        a, b = size * i, min(size * (i + 1), n)
                        return a, b, place[:, i % 2, 0:WIN * (b - a)].rearrange("p (b t) -> p b t", b=WIN)

                    def add(i):
                        a, b, p3 = places(i)
                        if i >= 2:
                            done(summed[i - 2])
                        added[i] = mark(V.tensor_tensor(
                            p3, count3[:, :, a:b], base[:].unsqueeze(2).to_broadcast([EP, WIN, b - a]), ALU.add))

                    if i == 0:
                        add(0)
                    a, b, p3 = places(i)
                    done(added[i])
                    picked = mark(V.tensor_tensor(p3, p3, win3[:, :, a:b], ALU.mult))
                    if i + 1 < SUMS:
                        add(i + 1)
                    done(picked)
                    summed[i] = mark(V.tensor_reduce(slot[:, a:b], p3.rearrange("p b t -> p t b"), AX.X, ALU.add))
                elif part == SLOTS:
                    done(summed[SUMS - 1])
                    scaled_round(col_s[:, 0:n], slot_t[:, 0:n], slot[:, 0:n], 1.0 / SLOT, -(SLOT / 2 + 0.5) / SLOT)
                    then(V.tensor_copy(col2[:, 0:n, :], twice(col_s[:, 0:n])))
                    then(V.scalar_tensor_tensor(slot[:, 0:n], col_s[:, 0:n], -float(SLOT), slot[:, 0:n],
                                                ALU.mult, ALU.add))
                    then(V.tensor_copy(row2[:, 0:n, :], twice(slot[:, 0:n])))
                elif part == WINDOW:
                    dve.wait_ge(window_ready, k + 1)
                    then(V.tensor_scalar(p_at[0:1, t0:t0 + c], sort_ps[0:1, 128:128 + c], float(SPLITS * HID),
                                         None, ALU.mult))
                    V.tensor_scalar(agg_at[0:1, t0:t0 + c], sort_ps[0:1, 128:128 + c], float(LO), None,
                                    ALU.mult).then_inc(slots_ready, 1)
                    dve.wait_ge(slots_ready, k + 1)

            def split2(ap):
                return ap.rearrange("p v (a b) -> p v a b", b=2)

            def sort_batch(k, n, j, q, m, late, between=None):
                c = TILES[k]
                if late:
                    dve.wait_ge(sort_mm, n - 1)

                def of(t, start, size, v):
                    if isinstance(start, int):
                        return t[:, start:start + size].rearrange("p t e -> p (t e)")
                    return t[:].rearrange("p t e -> p (t e)")[:, bass.ds(start * v, size * v)]

                def against(t, start, size, v, width):
                    return of(t, start, size, v).rearrange("p (a b) -> p a b", b=2).unsqueeze(2) \
                        .to_broadcast([EP, size * v // 2, width // 2, 2])

                def iota(t, width):
                    return t[0:EP, 0:width].rearrange("p (a b) -> p a b", b=2).unsqueeze(1) \
                        .to_broadcast([EP, m, width // 2, 2])

                V.tensor_tensor(split2(col_hot[:, q, 0:m, 0:c]), iota(iota0_b, c), against(col2, j, m, 2, c),
                                ALU.is_equal).then_inc(cols_ready, 1)
                V.tensor_tensor(split2(row_hot[:, q, 0:m, :]), iota(iota1_b, SLOT), against(row2, j, m, 2, SLOT),
                                ALU.is_equal).then_inc(hots_ready, 1)
                if between is not None:
                    place_weights(*between)
                dve.wait_ge(cols_ready, n + 1)
                cols = split2(col_hot[:, q, 0:m, 0:c])
                for t, payload, values in ((key_hot, key_in2, 2), (weight_hot, weight_in3, SPLITS)):
                    at = of(payload, j + COL0[k], m, 2 * values).rearrange("p (b v e) -> p b v e", b=m, v=values)
                    for v in range(values):
                        V.tensor_tensor(split2(t[:, q, 0:m, v, 0:c]), cols,
                                        at[:, :, v, :].unsqueeze(2).to_broadcast([EP, m, c // 2, 2]),
                                        ALU.mult).then_inc(hots_ready, 1)

            key_in2 = key_in[:].rearrange("p t v e -> p t (v e)")
            weight_in3 = weight_in[:].rearrange("p t v e -> p t (v e)")

            def read_sorted(k):
                c, t0 = TILES[k], GT * GRP0[k]
                dve.wait_ge(sorted_ready, k + 1)
                then(V.tensor_copy(key_s[:, :, 0:c], sort_ps[:, 0:2 * c].rearrange("p (v c) -> p v c", v=2)))
                then(V.tensor_scalar(odd[:, 0:c], key_s[:, 1, 0:c], float(KEY), None, ALU.is_ge))
                then(V.scalar_tensor_tensor(q_index[:, t0:t0 + c], key_s[:, 0, 0:c], 2.0, odd[:, 0:c],
                                            ALU.mult, ALU.add))
                then(V.scalar_tensor_tensor(key_s[:, 1, 0:c], odd[:, 0:c], -float(KEY), key_s[:, 1, 0:c],
                                            ALU.mult, ALU.add))
                then(V.tensor_copy(lo2[:, t0:t0 + c, :], key_s[:, 1, 0:c].unsqueeze(2).to_broadcast([128, c, 2])))
                V.tensor_copy(w_parts[:, t0:t0 + c, :], weight_ps[:, 0:SPLITS * c].rearrange("p (v c) -> p c v", c=c)) \
                    .then_inc(tables_ready, 1)
                dve.wait_ge(tables_ready, k + 1)

            def one_hots(g, u, n):
                if n >= 2:
                    dve.wait_ge(hotT_ps_ready, g - 1)
                    dve.wait_ge(hot32_ready, g - 1)
                if isinstance(g, int):
                    lo_g = lo2[:, GT * g:GT * g + GT, :]
                else:
                    lo_g = lo2[:].rearrange("p t e -> p (t e)")[:, bass.ds(g * (GT * 2), GT * 2)] \
                        .rearrange("p (t e) -> p t e", e=2)
                V.tensor_tensor(split2(hot[:, u % 2]),
                                iota1_b[:].rearrange("p (a b) -> p a b", b=2).unsqueeze(1).to_broadcast([128, GT, 64, 2]),
                                lo_g.unsqueeze(2).to_broadcast([128, GT, 64, 2]), ALU.is_equal).then_inc(hot_ready, 1)

            def place_weights(g, u):
                if isinstance(g, int):
                    w_g = w_parts[:, GT * g:GT * g + GT, :]
                else:
                    w_g = w_parts[:].rearrange("p t s -> p (t s)")[:, bass.ds(g * (GT * SPLITS), GT * SPLITS)] \
                        .rearrange("p (t s) -> p t s", s=SPLITS)
                dve.wait_ge(hot_ready, 2 * g + 1)
                V.tensor_copy(hot[:, u % 2, :, LO:128], w_g).then_inc(hot_ready, 1)

            def add_segments(m):
                at = agg_at[0:1, GT * m:GT * m + GT] if isinstance(m, int) else agg_at[0:1, bass.ds(m * GT, GT)]
                windows = nc.values_load_multi_w_load_instructions(
                    at, engines=(ENG.DVE,), min_val=0, max_val=(WIN - 1) * LO,
                    skip_runtime_bounds_check_because="a window's number is a count of 24 comparisons")[1]
                dve.wait_ge(seg_ready, m + 1)
                for j in range(GT):
                    dve.wait_ge(agg_added, m * GT + (j + 1))
                    o = agg[j % 2][:, bass.ds(windows[j], LO)]
                    V.tensor_tensor(o, o, seg_ps[:, j * LO:(j + 1) * LO], ALU.add).then_inc(agg_added, 1)

            def step(g, u, n, k=None, batch=None, j=None, q=None, size=None, parts=()):
                one_hots(g, u, n)
                if batch is not None:
                    sort_batch(k, batch, j, q, size, True, (g, u))
                else:
                    place_weights(g, u)
                for part, i in parts:
                    place_part(k, part, i)
                if n >= 4:
                    add_segments(g - 4)

            dve.wait_ge(fills_ready, FILLS)
            for part, i in VECTOR_ALL:
                if part == OFFSET:
                    payload()
                if part == SUM and i == 0:
                    payload_end()
                place_part(0, part, i)
            dve.wait_ge(payload_in, 2 + SPLITS)
            loop = full_batches(0)
            for n in range(UNROLL):
                sort_batch(0, n, BATCH[0] * n, n % 2, BATCH[0], n >= 2)
            with dve.Fori(UNROLL, loop - (UNROLL - 1), UNROLL) as n:
                for q in range(UNROLL):
                    sort_batch(0, n + q, n * BATCH[0] + q * BATCH[0], q % 2, BATCH[0], True)
            for n in range(loop, MIXED[0]):
                sort_batch(0, n, BATCH[0] * n, n % 2, batch_size(0, n), True)
            read_sorted(0)
            for k in range(CHUNKS):
                g0, g1 = GRP0[k], GRP0[k] + TILES[k] // GT
                if k + 1 == CHUNKS:
                    with dve.Fori(g0, g1 - (UNROLL - 1), UNROLL) as g:
                        for u in range(UNROLL):
                            step(g + u, u, LATE)
                    continue
                for i, parts in enumerate(VECTOR_PLACES[k + 1]):
                    step(g0 + i, i % UNROLL, g0 + i, k + 1, parts=parts)
                g0 += len(VECTOR_PLACES[k + 1])
                loop, size = full_batches(k + 1), BATCH[k + 1]
                with dve.Fori(g0, g0 + loop - (UNROLL - 1), UNROLL) as g:
                    for u in range(UNROLL):
                        step(g + u, (g0 + u) % UNROLL, LATE, k + 1, g + (u + BAT0[k + 1] - g0),
                             g * size + (u - g0) * size, (BAT0[k + 1] + u) % 2, size)
                for i in range(loop, MIXED[k + 1]):
                    n = BAT0[k + 1] + i
                    step(g0 + i, (g0 + i) % UNROLL, LATE, k + 1, n, i * size, n % 2, batch_size(k + 1, i))
                g0 += MIXED[k + 1]
                step(g0, g0 % UNROLL, LATE)
                read_sorted(k + 1)
                for g in range(g0 + 1, g1):
                    step(g, g % UNROLL, LATE)
            for m in range(GROUPS - 4, GROUPS):
                add_segments(m)

            dve.wait_ge(agg_added, GT * GROUPS + 2)
            for b0, b1 in xt_spans:
                a = agg[0][:, b0 * LO:b1 * LO]
                V.tensor_tensor(a, a, agg[1][:, b0 * LO:b1 * LO], ALU.add).then_inc(agg_whole, 1)
            for n, (b0, b1) in enumerate(ln_spans):
                w = b1 - b0
                y3 = y_banks[n % 2][0:LO, 0:w * NF].rearrange("p (b f) -> p b f", b=w)
                dve.wait_ge(y_ready, n + 1)
                then(V.tensor_reduce(stat[:, 3, b0:b1], y3, AX.X, ALU.add))
                then(V.tensor_scalar(stat[:, 0, b0:b1], stat[:, 3, b0:b1], 1.0 / NF, None, ALU.mult))
                V.tensor_tensor(yc[:, b0:b1, :], y3, stat[:, 0, b0:b1].unsqueeze(2).to_broadcast([LO, w, NF]),
                                ALU.subtract).then_inc(y_read, 1)
                dve.wait_ge(y_read, n + 1)
            dve.wait_ge(ln_sd, 1)
            then(V.reciprocal(stat[:, 0, :], stat[:, 2, :]))
            for b0, b1 in ln_spans:
                V.tensor_tensor(yc[:, b0:b1, :], yc[:, b0:b1, :],
                                stat[:, 0, b0:b1].unsqueeze(2).to_broadcast([LO, b1 - b0, NF]),
                                ALU.mult).then_inc(ln_done, 1)


_INS = ["x", "src", "dst", "edge_weight1", "L0_gnn_eW1", "L0_gnn_eb1", "L0_gnn_eW2", "L0_gnn_eb2",
        "L0_gnn_nW1", "L0_gnn_nb1", "L0_gnn_nW2", "L0_gnn_nb2"]


def kernel(**inputs):
    import numpy as _np
    import concourse.bacc as _bacc
    from concourse import mybir as _mybir
    from concourse.bass_utils import run_bass_kernel_spmd as _run

    nc = _bacc.Bacc("TRN2", target_bir_lowering=False, num_devices=1)
    arrays, args = {}, []
    for name in _INS:
        a = _np.ascontiguousarray(inputs[name])
        arrays[f"in_{name}_dram"] = a
        args.append(nc.dram_tensor(f"in_{name}_dram", a.shape, _mybir.dt.from_np(a.dtype), kind="ExternalInput").ap())
    args.append(nc.dram_tensor("out_0_dram", (NODES, NF), _mybir.dt.float32, kind="ExternalOutput").ap())
    build(nc, *args)
    r = _run(nc, [arrays], core_ids=[0])
    return r.results[0]["out_0_dram"]
```
